# Optimizing a Trainium2 kernel written in Bass

```python
import numpy as np
import jax
import jax.numpy as jnp

def _softmax(x, axis=-1):
    return jax.nn.softmax(x, axis=axis)

def _gelu(x):
    return jax.nn.gelu(x, approximate=True)

def _silu(x):
    return jax.nn.silu(x)

def _sigmoid(x):
    return jax.nn.sigmoid(x)

def _layernorm(x, axis=-1, eps=1e-05):
    m = jnp.mean(x, axis=axis, keepdims=True)
    v = jnp.var(x, axis=axis, keepdims=True)
    return (x - m) / jnp.sqrt(v + eps)

def _scatter_add(tgt, idx, src, axis=0):
    return tgt.at[idx].add(src)

def _segment_sum(src, seg, n):
    return jax.ops.segment_sum(src, seg, n)
kernel_name = 'mk_adaln_ffn_d1_seqx_r4_ca6032'

def setup_inputs(seed: int=0):
    np.random.seed(seed)
    _w = jnp.asarray

    def _rec_inputs():
        import jax
        import jax.numpy as jnp
        _rk = jax.random.key(seed)
        x = -0.0003929 + 0.9999 * jax.random.normal(jax.random.fold_in(_rk, 1), (8, 512, 256), jnp.float32)
        _lenS = 512 - jax.random.randint(jax.random.fold_in(_rk, 7), (8,), 0, max(1, 512 // 4) + 1, jnp.int32)
        _lenS2 = 512 - jax.random.randint(jax.random.fold_in(_rk, 8), (8,), 0, max(1, 512 // 4) + 1, jnp.int32)
        cond_256 = -0.0209273 + 1.04763 * jax.random.normal(jax.random.fold_in(_rk, 11), (8, 64), jnp.float32)
        return (x, cond_256)
    x, cond_256 = _rec_inputs()

    def _L0_cond_setup():
        import jax, jax.numpy as jnp
        import numpy as np
        EPS = 1e-08

        def hamilton(q1, q2):
            w1, x1, y1, z1 = (q1[..., i, :] for i in range(4))
            w2, x2, y2, z2 = (q2[..., i, :] for i in range(4))
            w = w1 * w2 - x1 * x2 - y1 * y2 - z1 * z2
            x = w1 * x2 + x1 * w2 + y1 * z2 - z1 * y2
            y = w1 * y2 - x1 * z2 + y1 * w2 + z1 * x2
            z = w1 * z2 + x1 * y2 - y1 * x2 + z1 * w2
            return jnp.stack([w, x, y, z], axis=-2)

        def _normalize(q):
            return q / jnp.sqrt(jnp.sum(q * q, axis=0, keepdims=True) + EPS)
        key = jax.random.key(seed)
        k1, k2, k3, k4 = jax.random.split(key, 4)
        B, T, d_model = (4, 1024, 256)
        quat_dim = d_model // 4
        x = jax.random.normal(k1, (B, T, d_model), dtype=jnp.float32)
        q_left = jax.random.normal(k2, (4, quat_dim), dtype=jnp.float32)
        q_right = jax.random.normal(k3, (4, quat_dim), dtype=jnp.float32)
        spectral_gate = jax.random.uniform(k4, (1, 1, 1, quat_dim), dtype=jnp.float32)
        return {'x': x, 'q_left': q_left, 'q_right': q_right, 'spectral_gate': spectral_gate}
    _L0_cond_all = _L0_cond_setup()
    _L0_cond_in = {k: v for k, v in _L0_cond_all.items() if k in ('q_right', 'spectral_gate')}
    del _L0_cond_all

    def _L0_ffn_setup():
        import jax, jax.numpy as jnp
        import numpy as np
        D_IN, D_H, D_OUT = (256, 256, 256)
        D_MOE = 1024
        N_EXPERTS = 8
        TOP_K = 2
        key = jax.random.key(seed)
        ks = jax.random.split(key, 10)
        s = lambda d: 1.0 / np.sqrt(d)
        x = jax.random.normal(ks[0], (2, 512, D_IN), dtype=jnp.float32)
        W_in = jax.random.normal(ks[1], (D_IN, D_H), dtype=jnp.float32) * s(D_IN)
        b_in = jnp.zeros((D_H,), jnp.float32)
        W_gate = jax.random.normal(ks[2], (D_H, N_EXPERTS), dtype=jnp.float32) * s(D_H)
        b_gate = jnp.zeros((N_EXPERTS,), jnp.float32)
        W1 = jax.random.normal(ks[3], (N_EXPERTS, D_H, D_MOE), dtype=jnp.float32) * s(D_H)
        b1 = jnp.zeros((N_EXPERTS, D_MOE), jnp.float32)
        W2 = jax.random.normal(ks[4], (N_EXPERTS, D_MOE, D_H), dtype=jnp.float32) * s(D_MOE)
        b2 = jnp.zeros((N_EXPERTS, D_H), jnp.float32)
        W_out = jax.random.normal(ks[5], (D_H, D_OUT), dtype=jnp.float32) * s(D_H)
        b_out = jnp.zeros((D_OUT,), jnp.float32)
        return {'x': x, 'W_in': W_in, 'b_in': b_in, 'W_gate': W_gate, 'b_gate': b_gate, 'W1': W1, 'b1': b1, 'W2': W2, 'b2': b2, 'W_out': W_out, 'b_out': b_out}
    _L0_ffn_all = _L0_ffn_setup()
    _L0_ffn_in = {k: v for k, v in _L0_ffn_all.items() if k in ('W_in', 'b_in', 'W_gate', 'b_gate', 'W1', 'b1', 'W2', 'b2', 'W_out', 'b_out')}
    del _L0_ffn_all
    return {'x': x, 'cond_256': cond_256, 'L0_cond_q_right': _L0_cond_in['q_right'], 'L0_cond_spectral_gate': _L0_cond_in['spectral_gate'], 'L0_ffn_W_in': _L0_ffn_in['W_in'], 'L0_ffn_b_in': _L0_ffn_in['b_in'], 'L0_ffn_W_gate': _L0_ffn_in['W_gate'], 'L0_ffn_b_gate': _L0_ffn_in['b_gate'], 'L0_ffn_W1': _L0_ffn_in['W1'], 'L0_ffn_b1': _L0_ffn_in['b1'], 'L0_ffn_W2': _L0_ffn_in['W2'], 'L0_ffn_b2': _L0_ffn_in['b2'], 'L0_ffn_W_out': _L0_ffn_in['W_out'], 'L0_ffn_b_out': _L0_ffn_in['b_out']}

def reference(x, cond_256, L0_cond_q_right, L0_cond_spectral_gate, L0_ffn_W_in, L0_ffn_b_in, L0_ffn_W_gate, L0_ffn_b_gate, L0_ffn_W1, L0_ffn_b1, L0_ffn_W2, L0_ffn_b2, L0_ffn_W_out, L0_ffn_b_out):
    import jax
    import jax.numpy as jnp

    def _L0_cond_ref(x, q_left, q_right, spectral_gate):
        import jax, jax.numpy as jnp
        import numpy as np
        EPS = 1e-08

        def hamilton(q1, q2):
            w1, x1, y1, z1 = (q1[..., i, :] for i in range(4))
            w2, x2, y2, z2 = (q2[..., i, :] for i in range(4))
            w = w1 * w2 - x1 * x2 - y1 * y2 - z1 * z2
            x = w1 * x2 + x1 * w2 + y1 * z2 - z1 * y2
            y = w1 * y2 - x1 * z2 + y1 * w2 + z1 * x2
            z = w1 * z2 + x1 * y2 - y1 * x2 + z1 * w2
            return jnp.stack([w, x, y, z], axis=-2)

        def _normalize(q):
            return q / jnp.sqrt(jnp.sum(q * q, axis=0, keepdims=True) + EPS)
        B, T, d_model = x.shape
        quat_dim = d_model // 4
        x_quat = x.reshape(B, T, 4, quat_dim)
        x_spectral = jnp.fft.fft(x_quat, axis=1)
        x_filtered = jnp.fft.ifft(x_spectral * spectral_gate, axis=1).real.astype(x.dtype)
        q_left_n = _normalize(q_left)
        q_right_n = _normalize(q_right)
        conj_sign = jnp.array([1.0, -1.0, -1.0, -1.0], dtype=x.dtype)[:, None]
        q_right_conj = q_right_n * conj_sign
        x_right = hamilton(x_filtered, q_right_conj)
        x_rotated = hamilton(q_left_n, x_right)
        return x_rotated.reshape(B, T, d_model)

    def _L0_ffn_ref(x, W_in, b_in, W_gate, b_gate, W1, b1, W2, b2, W_out, b_out):
        import jax, jax.numpy as jnp
        import numpy as np
        D_IN, D_H, D_OUT = (256, 256, 256)
        D_MOE = 1024
        N_EXPERTS = 8
        TOP_K = 2
        B, S, _ = x.shape
        h = x @ W_in + b_in
        t = h.reshape(B * S, -1)
        logits = t @ W_gate + b_gate
        probs = jax.nn.softmax(logits, axis=-1)
        topv, topi = jax.lax.top_k(probs, TOP_K)
        topv = topv / jnp.sum(topv, axis=-1, keepdims=True)
        route = jnp.zeros_like(probs).at[jnp.arange(t.shape[0])[:, None], topi].set(topv)
        mid = jax.nn.relu(jnp.einsum('nd,edh->neh', t, W1) + b1)
        eout = jnp.einsum('neh,ehd->ned', mid, W2) + b2
        moe_out = jnp.einsum('ne,ned->nd', route, eout)
        out = moe_out.reshape(B, S, -1) @ W_out + b_out
        return out
    x = x + _L0_ffn_ref(_L0_cond_ref(x, cond_256, L0_cond_q_right, L0_cond_spectral_gate), L0_ffn_W_in, L0_ffn_b_in, L0_ffn_W_gate, L0_ffn_b_gate, L0_ffn_W1, L0_ffn_b1, L0_ffn_W2, L0_ffn_b2, L0_ffn_W_out, L0_ffn_b_out)
    return x

_drawn_inputs = setup_inputs


def setup_inputs(seed=0):
    import zlib

    import numpy as np

    out = dict(_drawn_inputs(seed))
    spreads = {'L0_ffn_b_in': (0.0, 0.1),
     'L0_ffn_b_gate': (0.0, 0.1),
     'L0_ffn_b1': (0.0, 0.1),
     'L0_ffn_b2': (0.0, 0.1),
     'L0_ffn_b_out': (0.0, 0.1)}
    factors = {}
    for name, (base, spread) in spreads.items():
        noise = np.random.default_rng([zlib.crc32(name.encode()), seed]).standard_normal(out[name].shape)
        drawn = base * np.exp(spread * noise) if base else spread * noise
        out[name] = jnp.asarray(drawn.astype(out[name].dtype))
    for name, factor in factors.items():
        out[name] = (out[name] * factor).astype(out[name].dtype)
    return out
```

```python
import concourse.bass as bass
from concourse import mybir
from contextlib import ExitStack

RMAX = bass.bass_isa.ReduceOp.max


def moe_program(nc, x, cond, q_right, gate, W_in, b_in, W_gate, b_gate, W1, b1, W2, b2, W_out, b_out, out):
    f32, f16, i32 = mybir.dt.float32, mybir.dt.float16, mybir.dt.int32
    ALU, ACT, AX = mybir.AluOpType, mybir.ActivationFunctionType, mybir.AxisListType
    P = 128
    N, D = x.shape
    E, _, F = W1.shape
    KD, KF = D // P, F // P
    NT = N // P
    K = 2
    TS = 256
    H = TS // P
    NTILE = (K * N + E * (TS - 1)) // TS
    NA = NTILE * H
    CH = D // 4
    NCOND = cond.shape[0]
    XG = 4
    HF = F // 2

    ybuf = nc.dram_tensor("y_by_choice", (K * N + NTILE * TS, D), f32, kind="Internal").ap()

    ctx = ExitStack()
    with ctx:
        def sb(name, shape, dt):
            return ctx.enter_context(nc.sbuf_tensor(name, shape, dt))

        def sem(name):
            return ctx.enter_context(nc.semaphore(name))

        bank = [ctx.enter_context(nc.psum_tensor(f"bank{i}", [P, 512], f32)) for i in range(8)]

        FB = [bank[i] for i in (0, 1, 6, 7)]
        XB = [bank[i] for i in (2, 3)]
        YB = [bank[i] for i in (4, 5)]

        w1s = sb("w1s", [P, E, 2, KD, F], f16)
        w2s = sb("w2s", [P, E, 2, KF, D], f16)
        ident = sb("ident", [P, P], f32)
        ones = sb("ones", [P, P], f32)
        ones16 = sb("ones16", [P, P], f16)
        before = sb("before", [P, P], f16)
        mask = sb("mask", [P, CH], f32)
        iota_row = sb("iota_row", [P, P], f32)
        iota_e = sb("iota_e", [P, E], f32)
        choice_id = sb("choice_id", [P, K, NT], f32)
        pad_row = sb("pad_row", [P, NA], f32)
        scan_keep = sb("scan_keep", [P, E, NT], f32)
        qsrc = sb("qsrc", [P, 4 + NCOND + 1], f32)
        winr = sb("winr", [P, KD, D], f32)
        wgr = sb("wgr", [P, KD, E], f32)
        brow = sb("brow", [E * KF + KD, P], f32)
        bgr = sb("bgr", [1, E], f32)
        b2b = sb("b2b", [P, E, D], f32)
        boutb = sb("boutb", [P, D], f32)
        wout = sb("wout", [P, KD, D], f32)
        lq = sb("lq", [P, 4, 4], f32)
        rq = sb("rq", [P, 4, 4], f32)
        coef = sb("coef", [P, 4, 4], f32)
        ctmp = sb("ctmp", [P, 4, 4], f32)
        nrm = sb("nrm", [P, 8, 2], f32)
        qsq = sb("qsq", [P, 16], f32)
        wefft = sb("wefft", [P, KD, D], f32)
        wg = sb("wg", [P, KD, E], f32)
        bT = sb("bT", [P, E * KF + KD], f32)
        bg = sb("bg", [P, E], f32)
        xt_sb = sb("xt_sb", [P, 2, KD, P], f32)
        last1 = w1s[:, E - 1].bitcast(f32).rearrange("p l k f -> p (l k f)")
        last2 = w2s[:, E - 1].bitcast(f32).rearrange("p l k f -> p (l k f)")
        lg, pr, t3 = (last2[:, i * NT * E:(i + 1) * NT * E].rearrange("p (t e) -> p t e", t=NT) for i in range(3))
        oh = last2[:, 3 * NT * E:5 * NT * E].rearrange("p (k t e) -> p k t e", k=K, t=NT)
        tot, incl, sv = (last2[:, i * NT * E:(i + 1) * NT * E].rearrange("p (e t) -> p e t", e=E) for i in (5, 6, 7))
        ohb = last1[:, 0:4 * P].rearrange("p (s c) -> p s c", s=4)
        oha = last1[:, 4 * P:4 * P + 4 * NA].rearrange("p (s c) -> p s c", s=4)
        rt = last1[:, 1024:1024 + KD * D].rearrange("p (k d) -> p k d", k=KD)
        binrep = last1[:, 1536:1536 + KD * P].rearrange("p (k d) -> p k d", k=KD)
        m16 = sb("m16", [P, E, NT], f16)
        mx = sb("mx", [P, 8, NT], f32)
        route = sb("route", [P, K, NT], f32)
        cnt = sb("cnt", [P, 6, E], f32)
        cnti = sb("cnti", [P, 2, E], i32)
        slot = sb("slot", [P, K, NT], f32)
        sloti = sb("sloti", [P, 3, K, NT], i32)
        slotab = sb("slotab", [P, 2, K, NT], f32)
        ptmp = sb("ptmp", [P, NA], f32)
        dst = sb("dst", [P, NA], i32)
        src = sb("src", [P, 2, NA], i32)
        tile_e = sb("tile_e", [1, NTILE], i32)
        te = sb("te", [1, 2, NTILE, E], f32)
        xss = sb("xss", [P, NT], f32)
        xmax = sb("xmax", [P, 2], f32)
        wss = sb("wss", [P, 1 + 3 * E], f32)
        st = sb("st", [P, 2 + 3 * E], f32)
        sti = sb("sti", [P, 2, 2 + 3 * E], i32)
        ex = sb("ex", [P, 2 + 3 * E], f32)
        pw = sb("pw", [P, 6, E], f32)
        pwi = sb("pwi", [P, 5, E], i32)
        sxi = sb("sxi", [P, 2], i32)
        sxk = sb("sxk", [P, 2], f32)
        b1p = sb("b1p", [P, E, KF], f32)
        b1sq = sb("b1sq", [P, E, KF], f32)
        junk = sb("junk", [P, 2048], f16)
        RAW = KD * F
        region = sb("region", [P, 4 * RAW + 2 * XG * D], f32)
        raw1 = region[:, 0:2 * RAW].rearrange("p (s k f) -> p s k f", s=2, k=KD)
        raw2 = region[:, 2 * RAW:4 * RAW].rearrange("p (s k f) -> p s k f", s=2, k=KF)
        xin = region[:, 4 * RAW:4 * RAW + 2 * XG * D].rearrange("p (s t d) -> p s t d", s=2, t=XG)

        def cut(n_floats, at=[0]):
            at[0] += n_floats
            return region[:, at[0] - n_floats:at[0]]

        gx = cut(2 * H * D).rearrange("p (s h d) -> p s h d", s=2, h=H)
        ysb = cut(2 * H * D).rearrange("p (s h d) -> p s h d", s=2, h=H)
        midf = cut(KF * TS).rearrange("p (b c) -> p b c", b=4)
        xs = cut(2 * KD * TS).bitcast(f16).rearrange("p (s l k t) -> p s l k t", s=2, l=2, k=KD)
        mids = cut(2 * KF * TS).bitcast(f16).rearrange("p (s l b c) -> p s l b c", s=2, l=2, b=4)
        CG = 4
        fin = w1s[:, 0:4].bitcast(f32).rearrange("p e l k f -> p (e l k f)")
        yin = fin[:, 0:2 * CG * K * D].rearrange("p (s t k d) -> p s t k d", s=2, t=CG, k=K)
        o1 = 2 * CG * K * D
        xfin = fin[:, o1:o1 + 2 * CG * D].rearrange("p (s t d) -> p s t d", s=2, t=CG)
        zz = w2s[:, 0:2].bitcast(f32).rearrange("p e l k f -> p (e l k f)")
        ztok = zz[:, 0:2 * D].rearrange("p (s d) -> p s d", s=2)
        zt = zz[:, 2 * D:4 * D].rearrange("p (s k t) -> p s k t", s=2, k=KD)
        y1r = zz[:, 4 * D:6 * D].rearrange("p (s d) -> p s d", s=2)
        xb = w2s[:, 2:4].bitcast(f32).rearrange("p e l k f -> p (e l k f)")[:, 0:4 * D].rearrange("p (s d) -> p s d", s=4)
        osb = w2s[:, 4:8].bitcast(f32).rearrange("p e l k f -> p (e l k f)")[:, 0:2 * CG * D].rearrange("p (s t d) -> p s t d", s=2, t=CG)

        s_q, s_win, s_small, s_late = sem("q_loaded"), sem("win_loaded"), sem("small_loaded"), sem("late_loaded")
        s_x = [sem(f"x_loaded{i}") for i in range(2)]
        s_w1 = [sem(f"w1_loaded{i}") for i in range(2)]
        s_w2 = [sem(f"w2_loaded{i}") for i in range(2)]
        s_const = sem("constants_ready")
        s_pc = sem("pool_chain")
        s_lr = sem("quaternion_tables_ready")
        s_dc = sem("dve_chain")
        s_ac = sem("act_chain")
        s_rep = sem("bias_replicas_ready")
        s_n2 = sem("norm_squares_ready")
        s_root = sem("norm_roots_ready")
        s_rt = sem("rotation_ready")
        s_btp = sem("biases_transposed")
        s_bt = sem("biases_copied")
        s_wep = sem("wefft_product")
        s_we = sem("wefft_copied")
        s_wgp = sem("gate_product")
        s_wg = sem("gate_copied")
        s_wsq = sem("weff_squared")
        s_xtp = sem("x_transposed")
        s_xt = sem("xt_copied")
        s_xsq = sem("x_squared")
        s_lgp = sem("logits_product")
        s_ml = sem("logits_less_max")
        s_exp = sem("exp_ready")
        s_m = sem("choices_ready")
        s_rank = sem("ranks_product")
        s_oh = sem("onehots_ready")
        s_ohu = sem("onehots_used")
        s_idx = sem("slot_map_ready")
        s_xm = sem("x_norm_ready")
        s_xa = sem("x_norm_max_ready")
        s_sq1, s_sq2 = sem("w1_squared"), sem("w2_squared")
        s_sp, s_s = sem("norms_product"), sem("powers_ready")
        s_fp = sem("fold_product")
        s_fh, s_fl = sem("fold_high"), sem("fold_low")
        s_b1p = sem("b1_product")
        s_w2h, s_w2l = sem("w2_high"), sem("w2_low")
        s_bsq, s_bsp = sem("b1_squared"), sem("b1_norm_product")
        s_tab = sem("tables_ready")
        s_g = [sem(f"rows_gathered{i}") for i in range(2)]
        s_tp = sem("rows_transposed")
        s_xh, s_xl = sem("rows_high"), sem("rows_low")
        s_mp = sem("mid_product")
        s_mf = sem("mid_relu")
        s_mh, s_mq = sem("mid_high"), sem("mid_split")
        s_yp, s_ys = sem("y_product"), sem("y_ready")
        s_sc = [sem(f"rows_scattered{i}") for i in range(2)]
        s_yi = [sem(f"pairs_loaded{i}") for i in range(2)]
        s_y1 = sem("first_choice_scaled")
        s_z = sem("choices_mixed")
        s_zp = sem("mix_transposed")
        s_zt = sem("mix_copied")
        s_op = sem("out_product")
        s_xb = sem("x_plus_bias")
        s_o = sem("out_ready")
        s_st = [sem(f"out_stored{i}") for i in range(2)]

        block = ctx.enter_context(nc.Block())

        x_t = x.rearrange("(t p) d -> p t d", p=P)
        out_t = out.rearrange("(t p) d -> p t d", p=P)
        y_t = ybuf[0:K * N, :].rearrange("(t p k) d -> p t k d", p=P, k=K)
        NG = NT // XG
        NCG = NT // CG

        def mix_copy(act, t):
            act.wait_ge(s_zp, t + 1)
            if t >= 2:
                act.wait_ge(s_op, t - 1)
            nc.scalar.activation(zt[:, t % 2].rearrange("p k t -> p (k t)"), bank[t % 2][:, 0:D],
                                 ACT.Copy).then_inc(s_zt, 1)

        @block.sync
        def _(sp):
            for half in range(2):
                rows = slice(half * CH, (half + 1) * CH)
                with nc.allow_non_contiguous_dma(reason="a few hundred words, one per channel"):
                    sp.dma_start(qsrc[rows, 0:4], q_right.rearrange("c q -> q c")).then_inc(s_q, 16)
                    sp.dma_start(qsrc[rows, 4:4 + NCOND], cond.rearrange("c q -> q c")).then_inc(s_q, 16)
                    sp.dma_start(qsrc[rows, 4 + NCOND:5 + NCOND], gate.rearrange("c q -> q c")).then_inc(s_q, 16)
            sp.dma_start(winr[:], W_in.rearrange("(k p) n -> p k n", p=P)).then_inc(s_win, 16)
            sp.dma_start(wgr[:], W_gate.rearrange("(k p) n -> p k n", p=P)).then_inc(s_small, 16)
            sp.dma_start(brow[0:E * KF, :], b1.rearrange("e (c p) -> (e c) p", p=P)).then_inc(s_small, 16)
            sp.dma_start(brow[E * KF:E * KF + KD, :], b_in.rearrange("(k p) -> k p", p=P)).then_inc(s_small, 16)
            sp.dma_start(bgr[:], b_gate.rearrange("(a e) -> a e", a=1)).then_inc(s_small, 16)
            for g in range(NG):
                if g >= 2:
                    sp.wait_ge(s_xtp, XG * (g - 1))
                    sp.wait_ge(s_xsq, XG * (g - 1))
                sp.dma_start(xin[:, g % 2], x_t[:, g * XG:(g + 1) * XG, :]).then_inc(s_x[g % 2], 16)
                if g < 2:
                    sp.dma_start(raw1[:, g], W1[g].rearrange("(k p) f -> p k f", p=P)).then_inc(s_w1[g], 16)
                    sp.dma_start(raw2[:, g], W2[g].rearrange("(k p) f -> p k f", p=P)).then_inc(s_w2[g], 16)
            sp.dma_start(wout[:], W_out.rearrange("(k p) n -> p k n", p=P)).then_inc(s_late, 16)
            sp.dma_start(b2b[:].rearrange("p e d -> p (e d)"),
                         b2.rearrange("e d -> (e d)").partition_broadcast(P)).then_inc(s_late, 16)
            sp.dma_start(boutb[:], b_out.partition_broadcast(P)).then_inc(s_late, 16)
            for e in range(2, E):
                sp.wait_ge(s_b1p, e - 1)
                sp.wait_ge(s_sq1, e - 1)
                sp.dma_start(raw1[:, e % 2], W1[e].rearrange("(k p) f -> p k f", p=P)).then_inc(s_w1[e % 2], 16)
                sp.wait_ge(s_sq2, e - 1)
                sp.wait_ge(s_w2l, e - 1)
                sp.dma_start(raw2[:, e % 2], W2[e].rearrange("(k p) f -> p k f", p=P)).then_inc(s_w2[e % 2], 16)
            sp.wait_ge(s_sc[0], 16 * H * ((NTILE + 1) // 2))
            sp.wait_ge(s_sc[1], 16 * H * (NTILE // 2))
            for g in range(NCG):
                if g >= 2:
                    sp.wait_ge(s_z, CG * (g - 1))
                    sp.wait_ge(s_xb, CG * (g - 1))
                sp.dma_start(yin[:, g % 2], y_t[:, g * CG:(g + 1) * CG]).then_inc(s_yi[g % 2], 16)
                sp.dma_start(xfin[:, g % 2], x_t[:, g * CG:(g + 1) * CG, :]).then_inc(s_yi[g % 2], 16)
                if g >= 1:
                    sp.wait_ge(s_o, CG * g)
                    sp.dma_start(out_t[:, (g - 1) * CG:g * CG, :], osb[:, (g - 1) % 2]).then_inc(s_st[(g - 1) % 2], 16)
            sp.wait_ge(s_o, NT)
            sp.dma_start(out_t[:, NT - CG:NT, :], osb[:, (NCG - 1) % 2]).then_inc(s_st[(NCG - 1) % 2], 16)
            sp.wait_ge(s_st[0], 16 * ((NCG + 1) // 2))
            sp.wait_ge(s_st[1], 16 * (NCG // 2))

        @block.gpsimd
        def _(pool):
            chain = [0]

            def link(ins):
                chain[0] += 1
                ins.then_inc(s_pc, 1)
                pool.wait_ge(s_pc, chain[0])

            g = nc.gpsimd
            link(g.memset(ident[:], 0.0))
            g.affine_select(out=ident[:], in_=ident[:], compare_op=ALU.not_equal, fill=1.0, base=0,
                            pattern=[[-1, P]], channel_multiplier=1)
            link(g.memset(mask[:], 0.0))
            link(g.affine_select(out=mask[:], in_=mask[:], compare_op=ALU.not_equal, fill=1.0, base=0,
                                 pattern=[[-1, CH]], channel_multiplier=1))
            link(g.affine_select(out=mask[:], in_=mask[:], compare_op=ALU.not_equal, fill=1.0, base=-CH,
                                 pattern=[[-1, CH]], channel_multiplier=1))
            link(g.memset(before[:], 0.0))
            link(g.affine_select(out=before[:], in_=before[:], compare_op=ALU.is_ge, fill=1.0, base=0,
                                 pattern=[[-1, P]], channel_multiplier=1))
            g.memset(ones[:], 1.0)
            g.memset(ones16[:], 1.0)
            g.iota(iota_row[:], [[1, P]], base=0, channel_multiplier=0, allow_small_or_imprecise_dtypes=True)
            g.iota(iota_e[:], [[1, E]], base=-E, channel_multiplier=0, allow_small_or_imprecise_dtypes=True)
            g.iota(choice_id[:], [[1, K], [K * P, NT]], base=1, channel_multiplier=K,
                   allow_small_or_imprecise_dtypes=True)
            g.iota(pad_row[:], [[P, NA]], base=K * N + 1, channel_multiplier=1,
                   allow_small_or_imprecise_dtypes=True)
            link(g.memset(scan_keep[:], 1.0))
            g.memset(scan_keep[:, :, 0:1], 0.0).then_inc(s_const, 1)
            pool.wait_ge(s_q, 16 * 6)
            LQ = [[0, -1, -2, -3], [1, 0, -3, 2], [2, 3, 0, -1], [3, -2, 1, 0]]
            RQ = [[0, 1, 2, 3], [-1, 0, -3, 2], [-2, 3, 0, -1], [-3, -2, 1, 0]]
            for table, first, signs in ((lq, 4, LQ), (rq, 0, RQ)):
                for i in range(4):
                    for j in range(4):
                        q = signs[i][j]
                        last = g.tensor_scalar(table[:, i, j:j + 1], qsrc[:, first + abs(q):first + abs(q) + 1],
                                               -1.0 if q < 0 else 1.0, None, ALU.mult)
            last.then_inc(s_lr, 1)
            pool.wait_ge(s_xm, 1)
            g.partition_all_reduce(xmax[:, 1:2], xmax[:, 0:1], P, RMAX).then_inc(s_xa, 1)
            for e in range(E):
                pool.wait_ge(s_s, e + 1)
                pool.wait_ge(s_w2[e % 2], 16 * (e // 2 + 1))
                g.tensor_scalar(w2s[:, e, 0], raw2[:, e % 2], pwi[:, 1, e:e + 1].bitcast(f32), None,
                                ALU.mult).then_inc(s_w2h, 1)

            def gather(a, par, j, after):
                if after:
                    pool.wait_ge(s_tp, a - 1)
                for h in range(H):
                    g.indirect_dma_start(out=gx[:, par, h, :], out_offset=None, in_=x,
                                         in_offset=bass.IndirectOffsetOnAxis(ap=src_at(a, h), axis=0)
                                         ).then_inc(s_g[par], 16)

            def scatter(a, par):
                pool.wait_ge(s_ys, a + 1)
                for h in range(H):
                    g.indirect_dma_start(out=ybuf, out_offset=bass.IndirectOffsetOnAxis(ap=dst_at(a, h), axis=0),
                                         in_=ysb[:, par, h, :], in_offset=None).then_inc(s_sc[par], 16)

            def src_at(a, h):
                return src[:, 1, bass.ds(a * H + h, 1)]

            def dst_at(a, h):
                return dst[:, bass.ds(a * H + h, 1)]

            pool.wait_ge(s_idx, 1)
            pool.wait_ge(s_tab, 1)
            gather(0, 0, 0, False)
            gather(1, 1, 0, False)
            for a in range(NTILE):
                if a + 2 < NTILE:
                    gather(a + 2, a % 2, 0, True)
                scatter(a, a % 2)

        @block.scalar
        def _(act):
            s = nc.scalar
            act.wait_ge(s_n2, 1)
            s.activation(nrm[:, 1, :], nrm[:, 0, :], ACT.Sqrt).then_inc(s_root, 1)
            act.wait_ge(s_we, 1)
            s.activation(junk[:, 0:KD * D], wefft[:].rearrange("p k d -> p (k d)"), ACT.Square,
                         accum_out=wss[:, 0:1]).then_inc(s_wsq, 1)
            act.wait_ge(s_wsq, 1)
            for t in range(NT):
                if t % XG == 0:
                    act.wait_ge(s_x[(t // XG) % 2], 16 * (t // XG // 2 + 1))
                s.activation(junk[:, 1024 + (t % 2) * D:1024 + (t % 2 + 1) * D], xin[:, (t // XG) % 2, t % XG, :],
                             ACT.Square, accum_out=xss[:, t:t + 1]).then_inc(s_xsq, 1)
                if t >= 1:
                    act.wait_ge(s_xsq, t)
            act.wait_ge(s_ml, 1)
            s.activation(lg[:], t3[:], ACT.Exp).then_inc(s_exp, 1)

            def squares(e):
                act.wait_ge(s_w1[e % 2], 16 * (e // 2 + 1))
                if e:
                    act.wait_ge(s_sq2, e)
                s.activation(junk[:], raw1[:, e % 2].rearrange("p k f -> p (k f)"), ACT.Square,
                             accum_out=wss[:, 1 + e:2 + e]).then_inc(s_sq1, 1)
                act.wait_ge(s_w2[e % 2], 16 * (e // 2 + 1))
                act.wait_ge(s_sq1, e + 1)
                s.activation(junk[:], raw2[:, e % 2].rearrange("p k f -> p (k f)"), ACT.Square,
                             accum_out=wss[:, 1 + E + e:2 + E + e]).then_inc(s_sq2, 1)

            act.wait_ge(s_xsq, NT)
            squares(0)
            for e in range(E):
                if e + 1 < E:
                    squares(e + 1)
                act.wait_ge(s_s, e + 1)
                for i in range(4):
                    act.wait_ge(s_fp, 4 * e + i + 1)
                    s.activation(w1s[:, e, 0, i // 2, (i % 2) * HF:(i % 2 + 1) * HF], FB[i][:], ACT.Copy,
                                 scale=pwi[:, 0, e:e + 1].bitcast(f32)).then_inc(s_fh, 1)

            act.wait_ge(s_tab, 1)

            def rows_high(a, par):
                act.wait_ge(s_tp, a + 1)
                s.activation(xs[:, par, 0].rearrange("p k t -> p (k t)"), XB[par][:], ACT.Copy,
                             scale=sxi[:, 0:1].bitcast(f32)).then_inc(s_xh, 1)

            def relus(a, par, e, after):
                for b in range(4):
                    act.wait_ge(s_mp, 4 * a + b + 1)
                    if after:
                        act.wait_ge(s_mq, 4 * (a - 1) + b + 1)
                    for c in range(2):
                        m = s.activation(midf[:, b, c * TS:(c + 1) * TS], FB[b][:, c * TS:(c + 1) * TS], ACT.Relu,
                                         bias=b1s_at(e, 2 * b + c), scale=c1_at(e))
                    m.then_inc(s_mf, 1)

            def b1s_at(e, c):
                return b1p[:, bass.ds(e, 1), c:c + 1].rearrange("p e c -> p (e c)")

            def c1_at(e):
                return pwi[:, 2, bass.ds(e, 1)].bitcast(f32)

            def tile(a, par, first, last):
                e = act.value_load(tile_e[0:1, bass.ds(a, 1)], min_val=0, max_val=E - 1)
                relus(a, par, e, not first)
                if not last:
                    rows_high(a + 1, 1 - par)

            rows_high(0, 0)
            tile(0, 0, True, False)
            tile(1, 1, False, False)
            with act.Fori(1, NTILE // 2) as j:
                tile(j * 2, 0, False, False)
                tile(j * 2 + 1, 1, False, False)
            tile(NTILE - 1, 0, False, True)

            for t in range(NT):
                if t % CG == 0:
                    act.wait_ge(s_yi[(t // CG) % 2], 32 * (t // CG // 2 + 1))
                if t >= 2:
                    act.wait_ge(s_z, t - 1)
                s.activation(y1r[:, t % 2, :], yin[:, (t // CG) % 2, t % CG, 0, :], ACT.Copy,
                             scale=route[:, 0, t:t + 1]).then_inc(s_y1, 1)
                if t >= 1:
                    mix_copy(act, t - 1)
            mix_copy(act, NT - 1)

        @block.vector
        def _(dve):
            v = nc.vector
            chain = [0]

            def link(ins):
                chain[0] += 1
                ins.then_inc(s_dc, 1)
                dve.wait_ge(s_dc, chain[0])

            def bc(ap, shape):
                return ap.to_broadcast(shape)

            dve.wait_ge(s_q, 16 * 6)
            link(v.tensor_tensor(qsq[:, 0:4 + NCOND], qsrc[:, 0:4 + NCOND], qsrc[:, 0:4 + NCOND], ALU.mult))
            v.tensor_reduce(nrm[:, 2, 0:1], qsq[:, 0:4], AX.X, ALU.add)
            link(v.tensor_reduce(nrm[:, 2, 1:2], qsq[:, 4:4 + NCOND], AX.X, ALU.add))
            v.tensor_scalar(nrm[:, 0, :], nrm[:, 2, :], 1e-8, None, ALU.add).then_inc(s_n2, 1)
            dve.wait_ge(s_lr, 1)
            for m in range(4):
                to = coef if m == 0 else ctmp
                link(v.tensor_tensor(to[:], bc(lq[:, :, m:m + 1], [P, 4, 4]), bc(rq[:, m:m + 1, :], [P, 4, 4]),
                                     ALU.mult))
                if m:
                    link(v.tensor_tensor(coef[:], coef[:], ctmp[:], ALU.add))
            dve.wait_ge(s_root, 1)
            link(v.reciprocal(nrm[:, 3, :], nrm[:, 1, :]))
            link(v.tensor_tensor(nrm[:, 4, :], nrm[:, 3, :], nrm[:, 0, :], ALU.mult))
            link(v.tensor_tensor(nrm[:, 5, :], nrm[:, 4, :], nrm[:, 1, :], ALU.add))
            link(v.tensor_scalar(nrm[:, 6, :], nrm[:, 5, :], 0.5, None, ALU.mult))
            link(v.reciprocal(nrm[:, 7, :], nrm[:, 6, :]))
            link(v.tensor_tensor(qsq[:, 12:13], nrm[:, 7, 0:1], nrm[:, 7, 1:2], ALU.mult))
            link(v.tensor_tensor(qsq[:, 13:14], qsq[:, 12:13], qsrc[:, 4 + NCOND:5 + NCOND], ALU.mult))
            link(v.tensor_scalar(coef[:], coef[:], qsq[:, 13:14], None, ALU.mult))
            dve.wait_ge(s_const, 1)
            for k in range(KD):
                for half in range(2):
                    rows = slice(half * CH, (half + 1) * CH)
                    for ci in range(4):
                        last = v.tensor_scalar(rt[rows, k, ci * CH:(ci + 1) * CH], mask[rows, :],
                                               coef[rows, 2 * k + half, ci:ci + 1], None, ALU.mult)
            last.then_inc(s_rt, 1)
            dve.wait_ge(s_btp, 1)
            v.tensor_copy(bT[:], bank[2][:, 0:E * KF + KD]).then_inc(s_bt, 1)
            dve.wait_ge(s_wep, 1)
            v.tensor_copy(wefft[:].rearrange("p k d -> p (k d)"), bank[3][:]).then_inc(s_we, 1)
            dve.wait_ge(s_bt, 1)
            v.tensor_copy(binrep[:], bc(bT[:, E * KF:E * KF + KD].unsqueeze(2), [P, KD, P])).then_inc(s_rep, 1)
            dve.wait_ge(s_wgp, 1)
            v.tensor_copy(wg[:].rearrange("p k e -> p (k e)"), bank[4][:, 0:KD * E])
            v.tensor_copy(bg[:], bank[4][:, 64:64 + E]).then_inc(s_wg, 1)
            for t in range(NT):
                dve.wait_ge(s_xtp, t + 1)
                if t >= 2:
                    dve.wait_ge(s_lgp, t - 1)
                v.tensor_copy(xt_sb[:, t % 2].rearrange("p k t -> p (k t)"), bank[t % 2][:, 0:D]).then_inc(s_xt, 1)
            T3 = [P, NT, E]

            def col(i):
                return mx[:, i, :]

            def wide(i):
                return bc(mx[:, i, :].unsqueeze(2), T3)

            def ie():
                return bc(iota_e[:].unsqueeze(1), T3)

            dve.wait_ge(s_xsq, NT)
            v.tensor_reduce(xmax[:, 0:1], xss[:], AX.X, ALU.max).then_inc(s_xm, 1)
            dve.wait_ge(s_lgp, NT)
            dve.wait_ge(s_wg, 1)
            link(v.tensor_tensor(lg[:], bank[5][:, 0:NT * E].rearrange("p (t e) -> p t e", t=NT),
                                 bc(bg[:].unsqueeze(1), T3), ALU.add))
            link(v.tensor_reduce(col(0), lg[:], AX.X, ALU.max))
            v.tensor_tensor(t3[:], lg[:], wide(0), ALU.subtract).then_inc(s_ml, 1)
            dve.wait_ge(s_exp, 1)
            link(v.tensor_reduce(col(1), lg[:], AX.X, ALU.add))
            link(v.reciprocal(col(2), col(1)))
            link(v.tensor_tensor(pr[:], lg[:], wide(2), ALU.mult))
            for k in range(K):
                link(v.tensor_reduce(col(3 + k), pr[:], AX.X, ALU.max))
                link(v.tensor_tensor(t3[:], pr[:], wide(3 + k), ALU.is_equal))
                link(v.tensor_tensor(t3[:], t3[:], ie(), ALU.mult))
                link(v.tensor_reduce(col(5), t3[:], AX.X, ALU.min))
                link(v.tensor_tensor(oh[:, k], ie(), wide(5), ALU.is_equal))
                if k == 0:
                    link(v.scalar_tensor_tensor(pr[:], oh[:, 0], -2.0, pr[:], ALU.mult, ALU.add))
            v.tensor_tensor(m16[:].rearrange("p e t -> p t e"), oh[:, 0], oh[:, 1], ALU.add).then_inc(s_m, 1)
            link(v.tensor_tensor(col(5), col(3), col(4), ALU.add))
            link(v.reciprocal(col(6), col(5)))
            link(v.tensor_tensor(route[:], mx[:, 3:5, :], bc(mx[:, 6:7, :], [P, K, NT]), ALU.mult))
            dve.wait_ge(s_rank, 1)
            rk = bank[6][:].rearrange("p (s e t) -> p s e t", s=2, e=E)
            link(v.tensor_copy(tot[:], rk[:, 1]))
            link(v.tensor_tensor_scan(incl[:].rearrange("p e t -> p (e t)"), scan_keep[:].rearrange("p e t -> p (e t)"),
                                      tot[:].rearrange("p e t -> p (e t)"), 0.0, ALU.mult, ALU.add))
            link(v.tensor_scalar(cnti[:, 0, :], incl[:, :, NT - 1], float(TS - 1), None, ALU.add))
            link(v.tensor_scalar(cnti[:, 1, :], cnti[:, 0, :], TS.bit_length() - 1, None, ALU.logical_shift_right))
            link(v.tensor_copy(cnt[:, 0, :], cnti[:, 1, :]))
            link(v.tensor_tensor_scan(cnt[:, 1, :], ones[:, 0:E], cnt[:, 0, :], 0.0, ALU.mult, ALU.add))
            link(v.tensor_tensor(cnt[:, 2, :], cnt[:, 1, :], cnt[:, 0, :], ALU.subtract))
            link(v.tensor_scalar(cnt[:, 3, :], cnt[:, 2, :], float(TS), None, ALU.mult))
            link(v.tensor_tensor(sv[:], incl[:], tot[:], ALU.subtract))
            link(v.tensor_tensor(sv[:], sv[:], rk[:, 0], ALU.add))
            link(v.tensor_tensor(sv[:], sv[:], bc(cnt[:, 3, :].unsqueeze(2), [P, E, NT]), ALU.add))
            for k in range(K):
                link(v.tensor_tensor(t3[:], oh[:, k], sv[:].rearrange("p e t -> p t e"), ALU.mult))
                link(v.tensor_reduce(slot[:, k, :], t3[:], AX.X, ALU.add))
            link(v.tensor_copy(sloti[:, 0], slot[:]))
            link(v.tensor_scalar(sloti[:, 1], sloti[:, 0], P.bit_length() - 1, None, ALU.logical_shift_right))
            link(v.tensor_scalar(sloti[:, 2], sloti[:, 0], P - 1, None, ALU.bitwise_and))
            link(v.tensor_copy(slotab[:], sloti[:, 1:3]))
            for i in range(K * NT):
                k, t = divmod(i, NT)
                if i >= 4:
                    dve.wait_ge(s_ohu, i - 3)
                v.tensor_scalar(ohb[:, i % 4, :], iota_row[:], slotab[:, 1, k, t:t + 1], None, ALU.is_equal)
                v.tensor_scalar(oha[:, i % 4, :], iota_row[:, 0:NA], slotab[:, 0, k, t:t + 1],
                                choice_id[:, k, t:t + 1], ALU.is_equal, ALU.mult).then_inc(s_oh, 1)
            link(v.tensor_tensor(te[:, 0], bc(iota_row[0:1, 0:NTILE].unsqueeze(2), [1, NTILE, E]),
                                 bc(cnt[0:1, 1, :].unsqueeze(1), [1, NTILE, E]), ALU.is_ge))
            link(v.tensor_reduce(te[:, 1, :, 0], te[:, 0], AX.X, ALU.add))
            link(v.tensor_scalar(tile_e[:], te[:, 1, :, 0], float(E - 1), None, ALU.min))
            dve.wait_ge(s_ohu, K * NT)
            dmap = bank[7][:, 0:NA]
            link(v.scalar_tensor_tensor(ptmp[:], dmap, 0.0, pad_row[:], ALU.is_equal, ALU.mult))
            link(v.scalar_tensor_tensor(dst[:], dmap, -1.0, ptmp[:], ALU.add, ALU.add))
            link(v.tensor_scalar(src[:, 0, :], dmap, -1.0, 0.0, ALU.add, ALU.max))
            v.tensor_scalar(src[:, 1, :], src[:, 0, :], K.bit_length() - 1, None,
                            ALU.logical_shift_right).then_inc(s_idx, 1)

            def exponent(cols, have):
                if have is not None:
                    link(v.tensor_copy(st[:, cols], have))
                link(v.tensor_scalar(sti[:, 0, cols], st[:, cols].bitcast(i32), 23, None, ALU.logical_shift_right))
                link(v.tensor_scalar(sti[:, 1, cols], sti[:, 0, cols], -125.0, None, ALU.add))
                link(v.tensor_scalar(sti[:, 0, cols], sti[:, 1, cols], 1, None, ALU.arith_shift_right))
                link(v.tensor_scalar(ex[:, cols], sti[:, 0, cols], 1.0, None, ALU.mult))

            def power(bits, tmp, k):
                link(v.tensor_scalar(tmp, k, 126.0, -126.0, ALU.min, ALU.max))
                link(v.tensor_scalar(bits, tmp, 127.0, None, ALU.add))
                return v.tensor_scalar(bits, bits, 23, None, ALU.logical_shift_left)

            CW, C1, C2, CB, CX = 0, 1, 1 + E, 1 + 2 * E, 1 + 3 * E

            def clamp_k(to):
                link(v.tensor_scalar(to, to, 100.0, -100.0, ALU.min, ALU.max))

            def powers(e):
                dve.wait_ge(s_sp, e + 1)
                if e == 0:
                    exponent(slice(CW, CW + 1), bank[2][:, 128:129])
                exponent(slice(C1 + e, C1 + e + 1), bank[2][:, 129 + e:130 + e])
                exponent(slice(C2 + e, C2 + e + 1), bank[2][:, 129 + E + e:130 + E + e])
                link(v.tensor_scalar(pw[:, 0, e:e + 1], ex[:, C1 + e:C1 + e + 1], ex[:, CW:CW + 1], None, ALU.add))
                link(v.tensor_scalar(pw[:, 0, e:e + 1], pw[:, 0, e:e + 1], -1.0, 15.0, ALU.mult, ALU.add))
                link(v.tensor_scalar(pw[:, 1, e:e + 1], ex[:, C2 + e:C2 + e + 1], -1.0, 15.0, ALU.mult, ALU.add))
                clamp_k(pw[:, 0:2, e])
                power(pwi[:, 0:2, e], pw[:, 4:6, e], pw[:, 0:2, e]).then_inc(s_s, 1)

            for e in range(E):
                powers(e)
                dve.wait_ge(s_s, e + 1)
                for i in range(4):
                    dve.wait_ge(s_fh, 4 * e + i + 1)
                    v.scalar_tensor_tensor(w1s[:, e, 1, i // 2, (i % 2) * HF:(i % 2 + 1) * HF], FB[i][:],
                                           pwi[:, 0, e:e + 1].bitcast(f32),
                                           w1s[:, e, 0, i // 2, (i % 2) * HF:(i % 2 + 1) * HF],
                                           ALU.mult, ALU.subtract).then_inc(s_fl, 1)
                dve.wait_ge(s_w2h, e + 1)
                v.scalar_tensor_tensor(w2s[:, e, 1].rearrange("p k d -> p (k d)"),
                                       raw2[:, e % 2].rearrange("p k d -> p (k d)"), pwi[:, 1, e:e + 1].bitcast(f32),
                                       w2s[:, e, 0].rearrange("p k d -> p (k d)"),
                                       ALU.mult, ALU.subtract).then_inc(s_w2l, 1)
            dve.wait_ge(s_b1p, E)
            link(v.tensor_tensor(b1p[:].rearrange("p e c -> p (e c)"), bank[3][:, 0:E * KF], bT[:, 0:E * KF], ALU.add))
            link(v.tensor_tensor(b1sq[:], b1p[:], b1p[:], ALU.mult))
            v.tensor_reduce(wss[:, CB:CB + E], b1sq[:], AX.X, ALU.add).then_inc(s_bsq, 1)
            dve.wait_ge(s_bsp, 1)
            exponent(slice(CB, CB + E), bank[2][:, 160:160 + E])
            dve.wait_ge(s_xa, 1)
            link(v.tensor_copy(st[:, CX:CX + 1], xmax[:, 1:2]))
            exponent(slice(CX, CX + 1), None)
            link(v.tensor_scalar(sxk[:, 0:1], ex[:, CX:CX + 1], -1.0, 15.0, ALU.mult, ALU.add))
            clamp_k(sxk[:, 0:1])
            link(power(sxi[:, 0:1], sxk[:, 1:2], sxk[:, 0:1]))
            link(v.tensor_scalar(pw[:, 2, :], ex[:, C1:C1 + E], ex[:, CX:CX + 1], ex[:, CW:CW + 1], ALU.add, ALU.add))
            link(v.tensor_tensor(pw[:, 2, :], pw[:, 2, :], ex[:, CB:CB + E], ALU.max))
            link(v.tensor_scalar(pw[:, 2, :], pw[:, 2, :], -1.0, 14.0, ALU.mult, ALU.add))
            clamp_k(pw[:, 2, :])
            link(v.tensor_scalar(pw[:, 3, :], pw[:, 2, :], sxk[:, 0:1], None, ALU.subtract))
            link(v.tensor_tensor(pw[:, 3, :], pw[:, 3, :], pw[:, 0, :], ALU.subtract))
            link(power(pwi[:, 2, :], pw[:, 3, :], pw[:, 3, :]))
            link(v.tensor_tensor(pw[:, 3, :], pw[:, 2, :], pw[:, 1, :], ALU.add))
            link(v.tensor_scalar(pw[:, 3, :], pw[:, 3, :], -1.0, None, ALU.mult))
            link(power(pwi[:, 3, :], pw[:, 3, :], pw[:, 3, :]))
            link(power(pwi[:, 4, :], pw[:, 3, :], pw[:, 2, :]))
            dve.wait_ge(s_fl, 4 * E)
            dve.wait_ge(s_w2l, E)
            dve.wait_ge(s_late, 16 * 3)
            v.tensor_tensor(b1p[:], b1p[:], bc(pwi[:, 4, :].bitcast(f32).unsqueeze(2), [P, E, KF]),
                            ALU.mult).then_inc(s_tab, 1)

            def rows_low(a, par):
                dve.wait_ge(s_xh, a + 1)
                v.scalar_tensor_tensor(xs[:, par, 1].rearrange("p k t -> p (k t)"), XB[par][:],
                                       sxi[:, 0:1].bitcast(f32), xs[:, par, 0].rearrange("p k t -> p (k t)"),
                                       ALU.mult, ALU.subtract).then_inc(s_xl, 1)

            def split_mid(a, par):
                for b in range(4):
                    dve.wait_ge(s_mf, 4 * a + b + 1)
                    v.tensor_copy(mids[:, par, 0, b, :], midf[:, b, :]).then_inc(s_mh, 1)
                    dve.wait_ge(s_mh, 4 * a + b + 1)
                    v.tensor_tensor(mids[:, par, 1, b, :], midf[:, b, :], mids[:, par, 0, b, :],
                                    ALU.subtract).then_inc(s_mq, 1)

            def y_out(a, par, j, e, after):
                dve.wait_ge(s_yp, a + 1)
                if after:
                    dve.wait_ge(s_sc[par], j * (16 * H))
                for h in range(H):
                    last = v.scalar_tensor_tensor(ysb[:, par, h, :], YB[par][:, h * D:(h + 1) * D],
                                                  pwi[:, 3, bass.ds(e, 1)].bitcast(f32),
                                                  b2b[:, bass.ds(e, 1), :].rearrange("p e d -> p (e d)"),
                                                  ALU.mult, ALU.add)
                last.then_inc(s_ys, 1)

            def expert(a):
                return dve.value_load(tile_e[0:1, bass.ds(a, 1)], min_val=0, max_val=E - 1)

            rows_low(0, 0)
            split_mid(0, 0)
            rows_low(1, 1)
            split_mid(1, 1)
            rows_low(2, 0)
            y_out(0, 0, 0, expert(0), False)
            split_mid(2, 0)
            rows_low(3, 1)
            y_out(1, 1, 0, expert(1), False)
            split_mid(3, 1)
            rows_low(4, 0)
            y_out(2, 0, 1, expert(2), True)
            with dve.Fori(2, NTILE // 2) as j:
                split_mid(j * 2, 0)
                rows_low(j * 2 + 1, 1)
                y_out(j * 2 - 1, 1, j - 1, expert(j * 2 - 1), True)
                split_mid(j * 2 + 1, 1)
                rows_low(j * 2 + 2, 0)
                y_out(j * 2, 0, j, expert(j * 2), True)
            split_mid(NTILE - 1, 0)
            y_out(NTILE - 2, 1, (NTILE - 2) // 2, expert(NTILE - 2), True)
            y_out(NTILE - 1, 0, (NTILE - 1) // 2, expert(NTILE - 1), True)

            def finish(t):
                dve.wait_ge(s_op, t + 1)
                dve.wait_ge(s_xb, t + 1)
                if t >= 2 * CG:
                    dve.wait_ge(s_st[(t // CG) % 2], 16 * (t // CG // 2))
                v.tensor_tensor(osb[:, (t // CG) % 2, t % CG, :], bank[2 + t % 2][:, 0:D], xb[:, t % 4, :],
                                ALU.add).then_inc(s_o, 1)

            for t in range(NT):
                if t % CG == 0:
                    dve.wait_ge(s_yi[(t // CG) % 2], 32 * (t // CG // 2 + 1))
                if t >= 4:
                    dve.wait_ge(s_o, t - 3)
                v.tensor_tensor(xb[:, t % 4, :], xfin[:, (t // CG) % 2, t % CG, :], boutb[:], ALU.add).then_inc(s_xb, 1)
                dve.wait_ge(s_y1, t + 1)
                if t >= 2:
                    dve.wait_ge(s_zp, t - 1)
                v.scalar_tensor_tensor(ztok[:, t % 2, :], yin[:, (t // CG) % 2, t % CG, 1, :], route[:, 1, t:t + 1],
                                       y1r[:, t % 2, :], ALU.mult, ALU.add).then_inc(s_z, 1)
                if t >= 1:
                    finish(t - 1)
            finish(NT - 1)

        @block.tensor
        def _(pe):
            mm, tr = nc.tensor.matmul, nc.tensor.transpose
            NB = E * KF + KD
            pe.wait_ge(s_const, 1)
            pe.wait_ge(s_small, 16 * 4)
            tr(bank[2][:, 0:NB], brow[:], ident[0:NB, 0:NB]).then_inc(s_btp, 1)
            pe.wait_ge(s_rt, 1)
            pe.wait_ge(s_win, 16)
            for kd in range(KD):
                for kj in range(KD):
                    last = mm(bank[3][:, kd * D:(kd + 1) * D], winr[:, kj, kd * P:(kd + 1) * P], rt[:, kj, :],
                              start=(kj == 0), stop=(kj == KD - 1))
            last.then_inc(s_wep, 1)
            pe.wait_ge(s_we, 1)
            for ki in range(KD):
                for kd in range(KD):
                    mm(bank[4][:, ki * E:(ki + 1) * E], wefft[:, kd, ki * P:(ki + 1) * P], wgr[:, kd, :],
                       start=(kd == 0), stop=(kd == KD - 1))
            pe.wait_ge(s_rep, 1)
            for kd in range(KD):
                mm(bank[4][:, 64:64 + E], binrep[:, kd, :], wgr[:, kd, :], start=(kd == 0), stop=False)
            mm(bank[4][:, 64:64 + E], ones[0:1, :], bgr[:], start=False, stop=True).then_inc(s_wgp, 1)

            def logits(t):
                pe.wait_ge(s_xt, t + 1)
                for k in range(KD):
                    last = mm(bank[5][:, t * E:(t + 1) * E], xt_sb[:, t % 2, k, :], wg[:, k, :],
                              start=(k == 0), stop=(k == KD - 1))
                last.then_inc(s_lgp, 1)

            pe.wait_ge(s_wg, 1)
            for t in range(NT):
                if t % XG == 0:
                    pe.wait_ge(s_x[(t // XG) % 2], 16 * (t // XG // 2 + 1))
                if t >= 2:
                    pe.wait_ge(s_xt, t - 1)
                for k in range(KD):
                    last = tr(bank[t % 2][:, k * P:(k + 1) * P], xin[:, (t // XG) % 2, t % XG, k * P:(k + 1) * P],
                              ident[:])
                last.then_inc(s_xtp, 1)
                if t >= 1:
                    logits(t - 1)
            logits(NT - 1)
            pe.wait_ge(s_m, 1)
            m_et = m16[:].rearrange("p e t -> p (e t)")
            mm(bank[6][:, 0:E * NT], before[:], m_et, start=True, stop=True)
            mm(bank[6][:, E * NT:2 * E * NT], ones16[:], m_et, start=True, stop=True).then_inc(s_rank, 1)
            for i in range(K * NT):
                pe.wait_ge(s_oh, i + 1)
                mm(bank[7][:, 0:NA], ohb[:, i % 4, :], oha[:, i % 4, :], start=(i == 0),
                   stop=(i == K * NT - 1)).then_inc(s_ohu, 1)
            pe.wait_ge(s_idx, 1)
            for e in range(E):
                pe.wait_ge(s_wsq, 1)
                pe.wait_ge(s_sq2, e + 1)
                if e:
                    pe.wait_ge(s_s, e)
                if e == 0:
                    mm(bank[2][:, 128:129], ones[:], wss[:, 0:1], start=True, stop=True)
                mm(bank[2][:, 129 + e:130 + e], ones[:], wss[:, 1 + e:2 + e], start=True, stop=True)
                mm(bank[2][:, 129 + E + e:130 + E + e], ones[:], wss[:, 1 + E + e:2 + E + e], start=True,
                   stop=True).then_inc(s_sp, 1)
                pe.wait_ge(s_w1[e % 2], 16 * (e // 2 + 1))
                for i in range(4):
                    if e:
                        pe.wait_ge(s_fl, 4 * (e - 1) + i + 1)
                    for kd in range(KD):
                        last = mm(FB[i][:], wefft[:, kd, (i // 2) * P:(i // 2 + 1) * P],
                                  raw1[:, e % 2, kd, (i % 2) * HF:(i % 2 + 1) * HF],
                                  start=(kd == 0), stop=(kd == KD - 1))
                    last.then_inc(s_fp, 1)
                for c in range(KF):
                    for kd in range(KD):
                        last = mm(bank[3][:, e * KF + c:e * KF + c + 1], raw1[:, e % 2, kd, c * P:(c + 1) * P],
                                  bT[:, E * KF + kd:E * KF + kd + 1], start=(kd == 0), stop=(kd == KD - 1))
                last.then_inc(s_b1p, 1)
            pe.wait_ge(s_bsq, 1)
            pe.wait_ge(s_s, E)
            mm(bank[2][:, 160:160 + E], ones[:], wss[:, 1 + 2 * E:1 + 3 * E], start=True, stop=True).then_inc(s_bsp, 1)
            pe.wait_ge(s_tab, 1)

            def rows_t(a, par, j, after):
                pe.wait_ge(s_g[par], (j + 1) * (16 * H))
                if after:
                    pe.wait_ge(s_xl, a - 1)
                for k in range(KD):
                    for h in range(H):
                        last = tr(XB[par][:, k * TS + h * P:k * TS + (h + 1) * P], gx[:, par, h, k * P:(k + 1) * P],
                                  ident[:])
                last.then_inc(s_tp, 1)

            def w1_at(e, l, k, c):
                return w1s[:, bass.ds(e, 1), l, k, c * P:(c + 1) * P].rearrange("p e f -> p (e f)")

            def w2_at(e, l, c):
                return w2s[:, bass.ds(e, 1), l, c, :].rearrange("p e f -> p (e f)")

            def first_layer(a, par, e, after):
                pe.wait_ge(s_xl, a + 1)
                for b in range(4):
                    if after:
                        pe.wait_ge(s_mf, 4 * (a - 1) + b + 1)
                    for c in range(2):
                        o = FB[b][:, c * TS:(c + 1) * TS]
                        for k in range(KD):
                            w = w1_at(e, 0, k, 2 * b + c)
                            mm(o, w, xs[:, par, 0, k, :], start=(k == 0), stop=False)
                            mm(o, w, xs[:, par, 1, k, :], start=False, stop=False)
                            last = mm(o, w1_at(e, 1, k, 2 * b + c), xs[:, par, 0, k, :], start=False,
                                      stop=(k == KD - 1))
                    last.then_inc(s_mp, 1)

            def second_layer(a, par, e, after):
                if after:
                    pe.wait_ge(s_ys, a - 1)
                for b in range(4):
                    pe.wait_ge(s_mq, 4 * a + b + 1)
                    for c in range(2):
                        f = 2 * b + c
                        for l, w in ((0, 0), (1, 0), (0, 1)):
                            for h in range(H):
                                last = mm(YB[par][:, h * D:(h + 1) * D],
                                          mids[:, par, l, b, c * TS + h * P:c * TS + (h + 1) * P], w2_at(e, w, f),
                                          start=(f == 0 and l == 0 and w == 0 and h == 0),
                                          stop=(f == KF - 1 and w == 1), skip_group_check=True)
                last.then_inc(s_yp, 1)

            def expert(a):
                return pe.value_load(tile_e[0:1, bass.ds(a, 1)], min_val=0, max_val=E - 1)

            rows_t(0, 0, 0, False)
            first_layer(0, 0, expert(0), False)
            rows_t(1, 1, 0, False)
            first_layer(1, 1, expert(1), True)
            rows_t(2, 0, 1, True)
            second_layer(0, 0, expert(0), False)
            first_layer(2, 0, expert(2), True)
            rows_t(3, 1, 1, True)
            second_layer(1, 1, expert(1), False)
            first_layer(3, 1, expert(3), True)
            rows_t(4, 0, 2, True)
            second_layer(2, 0, expert(2), True)
            with pe.Fori(2, NTILE // 2) as j:
                first_layer(j * 2, 0, expert(j * 2), True)
                rows_t(j * 2 + 1, 1, j, True)
                second_layer(j * 2 - 1, 1, expert(j * 2 - 1), True)
                first_layer(j * 2 + 1, 1, expert(j * 2 + 1), True)
                rows_t(j * 2 + 2, 0, j + 1, True)
                second_layer(j * 2, 0, expert(j * 2), True)
            first_layer(NTILE - 1, 0, expert(NTILE - 1), True)
            second_layer(NTILE - 2, 1, expert(NTILE - 2), True)
            second_layer(NTILE - 1, 0, expert(NTILE - 1), True)

            def project(t):
                pe.wait_ge(s_zt, t + 1)
                if t >= 2:
                    pe.wait_ge(s_o, t - 1)
                for k in range(KD):
                    last = mm(bank[2 + t % 2][:, 0:D], zt[:, t % 2, k, :], wout[:, k, :], start=(k == 0),
                              stop=(k == KD - 1))
                last.then_inc(s_op, 1)

            for t in range(NT):
                pe.wait_ge(s_z, t + 1)
                if t >= 2:
                    pe.wait_ge(s_zt, t - 1)
                for k in range(KD):
                    last = tr(bank[t % 2][:, k * P:(k + 1) * P], ztok[:, t % 2, k * P:(k + 1) * P], ident[:])
                last.then_inc(s_zp, 1)
                if t >= 1:
                    project(t - 1)
            project(NT - 1)


_ARGS = ['x', 'cond_256', 'L0_cond_q_right', 'L0_cond_spectral_gate', 'L0_ffn_W_in', 'L0_ffn_b_in', 'L0_ffn_W_gate',
         'L0_ffn_b_gate', 'L0_ffn_W1', 'L0_ffn_b1', 'L0_ffn_W2', 'L0_ffn_b2', 'L0_ffn_W_out', 'L0_ffn_b_out']


def kernel(**inputs):
    import numpy as _np
    import concourse.bacc as _bacc
    from concourse import mybir as _mybir
    from concourse.bass_utils import run_bass_kernel_spmd as _run

    nc = _bacc.Bacc("TRN2", target_bir_lowering=False, num_devices=1)
    arrays, args = {}, []
    for name in _ARGS:
        a = _np.ascontiguousarray(inputs[name])
        if name == 'x':
            a = a.reshape(-1, a.shape[-1])
        if name == 'L0_cond_spectral_gate':
            a = a.reshape(1, -1)
        arrays[f"in_{name}"] = a
        args.append(nc.dram_tensor(f"in_{name}", a.shape, _mybir.dt.from_np(a.dtype), kind="ExternalInput").ap())
    shape = _np.shape(inputs['x'])
    out = nc.dram_tensor("out_0", (shape[0] * shape[1], shape[2]), _mybir.dt.float32, kind="ExternalOutput").ap()
    moe_program(nc, *args, out)
    r = _run(nc, [arrays], core_ids=[0])
    return r.results[0]["out_0"].reshape(shape)
```

```python
import concourse.bass as bass
from concourse import mybir
from contextlib import ExitStack

RMAX = bass.bass_isa.ReduceOp.max


def moe_program(nc, x, cond, q_right, gate, W_in, b_in, W_gate, b_gate, W1, b1, W2, b2, W_out, b_out, out):
    f32, f16, i32 = mybir.dt.float32, mybir.dt.float16, mybir.dt.int32
    ALU, ACT, AX = mybir.AluOpType, mybir.ActivationFunctionType, mybir.AxisListType
    P = 128
    N, D = x.shape
    E, _, F = W1.shape
    KD, KF = D // P, F // P
    NT = N // P
    K = 2
    TS = 256
    H = TS // P
    NTILE = (K * N + E * (TS - 1)) // TS
    NA = NTILE * H
    CH = D // 4
    NCOND = cond.shape[0]
    XG = 4
    OB = 8
    HF = F // 2

    ybuf = nc.dram_tensor("y_by_choice", (K * N + NTILE * TS, D), f32, kind="Internal").ap()

    ctx = ExitStack()
    with ctx:
        def sb(name, shape, dt):
            return ctx.enter_context(nc.sbuf_tensor(name, shape, dt))

        def sem(name):
            return ctx.enter_context(nc.semaphore(name))

        bank = [ctx.enter_context(nc.psum_tensor(f"bank{i}", [P, 512], f32)) for i in range(8)]

        FB = [bank[i] for i in (0, 1, 6, 7)]
        XB = [bank[i] for i in (2, 3)]
        YB = [bank[i] for i in (4, 5)]

        w1s = sb("w1s", [P, E, 2, KD, F], f16)
        w2s = sb("w2s", [P, E, 2, KF, D], f16)
        ident = sb("ident", [P, P], f32)
        ones = sb("ones", [P, P], f32)
        ones16 = sb("ones16", [P, P], f16)
        before = sb("before", [P, P], f16)
        mask = sb("mask", [P, CH], f32)
        iota_row = sb("iota_row", [P, P], f32)
        iota_e = sb("iota_e", [P, E], f32)
        choice_id = sb("choice_id", [P, K, NT], f32)
        pad_row = sb("pad_row", [P, NA], f32)
        scan_keep = sb("scan_keep", [P, E, NT], f32)
        qsrc = sb("qsrc", [P, 4 + NCOND + 1], f32)
        winr = sb("winr", [P, KD, D], f32)
        wgr = sb("wgr", [P, KD, E], f32)
        brow = sb("brow", [E * KF + KD, P], f32)
        bgr = sb("bgr", [1, E], f32)
        b2b = sb("b2b", [P, E, D], f32)
        boutb = sb("boutb", [P, D], f32)
        wout = sb("wout", [P, KD, D], f32)
        lq = sb("lq", [P, 4, 4], f32)
        rq = sb("rq", [P, 4, 4], f32)
        coef = sb("coef", [P, 4, 4], f32)
        ctmp = sb("ctmp", [P, 4, 4], f32)
        nrm = sb("nrm", [P, 8, 2], f32)
        qsq = sb("qsq", [P, 16], f32)
        wefft = sb("wefft", [P, KD, D], f32)
        wg = sb("wg", [P, KD, E], f32)
        bT = sb("bT", [P, E * KF + KD], f32)
        bg = sb("bg", [P, E], f32)
        last1 = w1s[:, E - 1].bitcast(f32).rearrange("p l k f -> p (l k f)")
        last2 = w2s[:, E - 1].bitcast(f32).rearrange("p l k f -> p (l k f)")
        lg, pr, t3 = (last2[:, i * NT * E:(i + 1) * NT * E].rearrange("p (t e) -> p t e", t=NT) for i in range(3))
        oh = last2[:, 3 * NT * E:5 * NT * E].rearrange("p (k t e) -> p k t e", k=K, t=NT)
        tot, incl, sv = (last2[:, i * NT * E:(i + 1) * NT * E].rearrange("p (e t) -> p e t", e=E) for i in (5, 6, 7))
        ohb = w1s[:, E - 1].bitcast(f32).rearrange("p l k f -> p (l k f)").rearrange("p (s i c) -> p s i c", s=2, i=OB)
        oha = sb("oha", [P, 2, OB, NA], f32)
        rt = last1[:, 0:KD * D].rearrange("p (k d) -> p k d", k=KD)
        binrep = last1[:, 512:512 + KD * P].rearrange("p (k d) -> p k d", k=KD)
        xt_sb = last1[:, 1024:2048].rearrange("p (s t k c) -> p s t k c", s=2, t=2, k=KD)
        m16 = sb("m16", [P, E, NT], f16)
        mx = sb("mx", [P, 8, NT], f32)
        route = sb("route", [P, K, NT], f32)
        cnt = sb("cnt", [P, 6, E], f32)
        cnti = sb("cnti", [P, 2, E], i32)
        slot = sb("slot", [P, K, NT], f32)
        sloti = sb("sloti", [P, 3, K, NT], i32)
        slotab = sb("slotab", [P, 2, K, NT], f32)
        ptmp = sb("ptmp", [P, NA], f32)
        dst = sb("dst", [P, NA], i32)
        src = sb("src", [P, 2, NA], i32)
        tile_e = sb("tile_e", [1, NTILE], i32)
        te = sb("te", [1, 2, NTILE, E], f32)
        xss = sb("xss", [P, NT // XG], f32)
        xmax = sb("xmax", [P, 2], f32)
        wss = sb("wss", [P, E, 2], f32)
        oss = sb("oss", [P, 1 + E], f32)
        fw2 = sb("fw2", [P, 2], f32)
        sq = sb("sq", [P, E, 2], f32)
        hw = sb("hw", [P, E, 2], i32)
        hk = sb("hk", [P, E, 2], i32)
        s12 = sb("s12", [P, E, 2], i32)
        sqo = sb("sqo", [P, 1 + E], f32)
        ho = sb("ho", [P, 1 + E], i32)
        sx = sb("sx", [P, 2], i32)
        hf = sb("hf", [P, 3, 1 + 2 * E], f32)
        kk = sb("kk", [P, 6, E], f32)
        cbits = sb("cbits", [P, 3, 2, E], i32)
        b1p = sb("b1p", [P, E, KF], f32)
        b1sq = sb("b1sq", [P, E, KF], f32)
        junk = sb("junk", [P, 2048], f16)
        xj = w2s[:, E - 2, 0].rearrange("p k d -> p (k d)")[:, 0:XG * D]
        RAW = KD * F
        region = sb("region", [P, 4 * RAW + 2 * XG * D], f32)
        raw1 = region[:, 0:2 * RAW].rearrange("p (s k f) -> p s k f", s=2, k=KD)
        raw2 = region[:, 2 * RAW:4 * RAW].rearrange("p (s k f) -> p s k f", s=2, k=KF)
        xin = region[:, 4 * RAW:4 * RAW + 2 * XG * D].rearrange("p (s t d) -> p s t d", s=2, t=XG)

        gx = region[:, 4 * RAW:4 * RAW + 2 * H * D].rearrange("p (s h d) -> p s h d", s=2, h=H)
        ysb = region[:, 4 * RAW + 2 * H * D:4 * RAW + 4 * H * D].rearrange("p (s h d) -> p s h d", s=2, h=H)
        midf = region[:, 0:KF * TS].rearrange("p (b c) -> p b c", b=4)
        xs = region[:, KF * TS:(KF + 2 * KD) * TS].bitcast(f16).rearrange("p (s l k t) -> p s l k t", s=2, l=2, k=KD)
        mids = region[:, (KF + 2 * KD) * TS:(3 * KF + 2 * KD) * TS].bitcast(f16).rearrange(
            "p (s l b c) -> p s l b c", s=2, l=2, b=4)
        CT = 2
        NS = NT // CT
        SL = 4
        fin = w1s[:].bitcast(f32).rearrange("p e l k f -> p (e l k f)")

        def fin_cut(at, n, pattern, **sizes):
            return fin[:, at * D:(at + n) * D].rearrange(pattern, **sizes)

        yin = fin_cut(0, SL * CT * K, "p (s t k d) -> p s t k d", s=SL, t=CT, k=K)
        xfin = fin_cut(16, SL * CT, "p (s t d) -> p s t d", s=SL, t=CT)
        xb = fin_cut(24, SL * CT, "p (s t d) -> p s t d", s=SL, t=CT)
        osb = fin_cut(32, SL * CT, "p (s t d) -> p s t d", s=SL, t=CT)
        ztok = fin_cut(40, 2 * CT, "p (s t d) -> p s t d", s=2, t=CT)
        y1r = fin_cut(44, 2 * CT, "p (s t d) -> p s t d", s=2, t=CT)
        zt = fin_cut(48, 2 * CT, "p (s t k c) -> p s t k c", s=2, t=CT, k=KD)

        s_q, s_win, s_small, s_late = sem("q_loaded"), sem("win_loaded"), sem("small_loaded"), sem("late_loaded")
        s_x = [sem(f"x_loaded{i}") for i in range(2)]
        s_w1 = [sem(f"w1_loaded{i}") for i in range(2)]
        s_w2 = [sem(f"w2_loaded{i}") for i in range(2)]
        s_const = sem("constants_ready")
        s_pc = sem("pool_chain")
        s_lr = sem("quaternion_tables_ready")
        s_dc = sem("dve_chain")
        s_ac = sem("act_chain")
        s_rep = sem("bias_replicas_ready")
        s_n2 = sem("norm_squares_ready")
        s_root = sem("norm_roots_ready")
        s_rt = sem("rotation_ready")
        s_btp = sem("biases_transposed")
        s_bt = sem("biases_copied")
        s_wep = sem("wefft_product")
        s_we = sem("wefft_copied")
        s_wgp = sem("gate_product")
        s_wg = sem("gate_copied")
        s_wsq = sem("weff_squared")
        s_xtp = sem("x_transposed")
        s_xt = sem("xt_copied")
        s_xsq = sem("x_squared")
        s_lgp = sem("logits_product")
        s_ml = sem("logits_less_max")
        s_exp = sem("exp_ready")
        s_m = sem("choices_ready")
        s_rank = sem("ranks_product")
        s_ohe = sem("onehots_compared")
        s_oh = sem("onehots_ready")
        s_ohu = sem("onehots_used")
        s_ohp = sem("onehots_multiplied")
        s_wnp, s_wn = sem("weff_norm_product"), sem("weff_norm_ready")
        s_idx = sem("slot_map_ready")
        s_xm = sem("x_norm_ready")
        s_xa = sem("x_norm_max_ready")
        s_sq1, s_sq2 = sem("w1_squared"), sem("w2_squared")
        s_sp, s_s = sem("norms_product"), sem("powers_ready")
        s_fp = sem("fold_product")
        s_fh, s_fl = sem("fold_high"), sem("fold_low")
        s_b1p = sem("b1_product")
        s_w2h, s_w2l = sem("w2_high"), sem("w2_low")
        s_bsq, s_bsp = sem("b1_squared"), sem("b1_norm_product")
        s_tab = sem("tables_ready")
        s_g = [sem(f"rows_gathered{i}") for i in range(2)]
        s_tp = sem("rows_transposed")
        s_xh, s_xl = sem("rows_high"), sem("rows_low")
        s_mp = sem("mid_product")
        s_mf = sem("mid_relu")
        s_mh, s_mq = sem("mid_high"), sem("mid_split")
        s_yp, s_ys = sem("y_product"), sem("y_ready")
        s_sc = [sem(f"rows_scattered{i}") for i in range(2)]
        s_yi = [sem(f"pairs_loaded{i}") for i in range(SL)]
        s_y1 = sem("first_choice_scaled")
        s_z = sem("choices_mixed")
        s_zp = sem("mix_transposed")
        s_zt = sem("mix_copied")
        s_op = sem("out_product")
        s_xb = sem("x_plus_bias")
        s_o = sem("out_ready")
        s_st = [sem(f"out_stored{i}") for i in range(SL)]

        block = ctx.enter_context(nc.Block())

        x_t = x.rearrange("(t p) d -> p t d", p=P)
        out_t = out.rearrange("(t p) d -> p t d", p=P)
        y_t = ybuf[0:K * N, :].rearrange("(t p k) d -> p t k d", p=P, k=K)
        NG = NT // XG
        NB = NT * K // OB

        def later(i, n):
            return not isinstance(i, int) or i >= n

        def tiles(eng, step):
            for a in range(4):
                step(a, a % 2, a // 2)
            with eng.Fori(2, NTILE // 2) as j:
                step(j * 2, 0, j)
                step(j * 2 + 1, 1, j)
            step(NTILE - 1, 0, NTILE // 2)

        def combine(eng, step):
            for i in range(SL):
                step(i, i, 0)
            with eng.Fori(1, NS // SL) as j:
                for q in range(SL):
                    step(j * SL + q, q, j)

        @block.sync
        def _(sp):
            for half in range(2):
                rows = slice(half * CH, (half + 1) * CH)
                with nc.allow_non_contiguous_dma(reason="a few hundred words, one per channel"):
                    sp.dma_start(qsrc[rows, 0:4], q_right.rearrange("c q -> q c")).then_inc(s_q, 16)
                    sp.dma_start(qsrc[rows, 4:4 + NCOND], cond.rearrange("c q -> q c")).then_inc(s_q, 16)
                    sp.dma_start(qsrc[rows, 4 + NCOND:5 + NCOND], gate.rearrange("c q -> q c")).then_inc(s_q, 16)
            sp.dma_start(winr[:], W_in.rearrange("(k p) n -> p k n", p=P)).then_inc(s_win, 16)
            sp.dma_start(wgr[:], W_gate.rearrange("(k p) n -> p k n", p=P)).then_inc(s_small, 16)
            sp.dma_start(brow[0:E * KF, :], b1.rearrange("e (c p) -> (e c) p", p=P)).then_inc(s_small, 16)
            sp.dma_start(brow[E * KF:E * KF + KD, :], b_in.rearrange("(k p) -> k p", p=P)).then_inc(s_small, 16)
            sp.dma_start(bgr[:], b_gate.rearrange("(a e) -> a e", a=1)).then_inc(s_small, 16)

            def load_x(g):
                if g >= 2:
                    sp.wait_ge(s_xtp, XG // 2 * (g - 1))
                    sp.wait_ge(s_xsq, g - 1)
                sp.dma_start(xin[:, g % 2], x_t[:, g * XG:(g + 1) * XG, :]).then_inc(s_x[g % 2], 16)

            def load_w1(e):
                if e >= 2:
                    sp.wait_ge(s_b1p, e - 1)
                    sp.wait_ge(s_sq1, e - 1)
                sp.dma_start(raw1[:, e % 2], W1[e].rearrange("(k p) f -> p k f", p=P)).then_inc(s_w1[e % 2], 16)

            def load_w2(e):
                if e >= 2:
                    sp.wait_ge(s_sq2, e - 1)
                    sp.wait_ge(s_w2l, e - 1)
                sp.dma_start(raw2[:, e % 2], W2[e].rearrange("(k p) f -> p k f", p=P)).then_inc(s_w2[e % 2], 16)

            load_x(0)
            load_w1(0)
            load_x(1)
            load_w2(0)
            load_w1(1)
            load_w2(1)
            for g in range(2, NG):
                load_x(g)
                if g % 2 and g // 2 + 1 < NG // 2:
                    load_w1(g // 2 + 1)
                    load_w2(g // 2 + 1)
            sp.dma_start(wout[:], W_out.rearrange("(k p) n -> p k n", p=P)).then_inc(s_late, 16)
            sp.dma_start(b2b[:].rearrange("p e d -> p (e d)"),
                         b2.rearrange("e d -> (e d)").partition_broadcast(P)).then_inc(s_late, 16)
            sp.dma_start(boutb[:], b_out.partition_broadcast(P)).then_inc(s_late, 16)
            for e in range(NG // 2, E):
                load_w1(e)
                load_w2(e)
            sp.wait_ge(s_sc[0], 16 * H * ((NTILE + 1) // 2))
            sp.wait_ge(s_sc[1], 16 * H * (NTILE // 2))

            def load(i, slot):
                if later(i, SL):
                    sp.wait_ge(s_z, i - (SL - 1))
                    sp.wait_ge(s_xb, i - (SL - 1))
                sp.dma_start(yin[:, slot], y_t[:, bass.ds(i * CT, CT)]).then_inc(s_yi[slot], 16)
                sp.dma_start(xfin[:, slot], x_t[:, bass.ds(i * CT, CT), :]).then_inc(s_yi[slot], 16)

            def store(i, slot):
                sp.wait_ge(s_o, i + 1)
                sp.dma_start(out_t[:, bass.ds(i * CT, CT), :], osb[:, slot]).then_inc(s_st[slot], 16)

            for i in range(SL):
                load(i, i)
            with sp.Fori(0, NS // SL - 1) as j:
                for q in range(SL):
                    load(j * SL + (q + SL), q)
                    store(j * SL + q, q)
            for i in range(NS - SL, NS):
                store(i, i % SL)
            for slot in range(SL):
                sp.wait_ge(s_st[slot], 16 * (NS // SL))

        @block.gpsimd
        def _(pool):
            chain = [0]

            def link(ins):
                chain[0] += 1
                ins.then_inc(s_pc, 1)
                pool.wait_ge(s_pc, chain[0])

            g = nc.gpsimd
            link(g.memset(ident[:], 0.0))
            g.affine_select(out=ident[:], in_=ident[:], compare_op=ALU.not_equal, fill=1.0, base=0,
                            pattern=[[-1, P]], channel_multiplier=1)
            link(g.memset(mask[:], 0.0))
            link(g.affine_select(out=mask[:], in_=mask[:], compare_op=ALU.not_equal, fill=1.0, base=0,
                                 pattern=[[-1, CH]], channel_multiplier=1))
            link(g.affine_select(out=mask[:], in_=mask[:], compare_op=ALU.not_equal, fill=1.0, base=-CH,
                                 pattern=[[-1, CH]], channel_multiplier=1))
            link(g.memset(before[:], 0.0))
            link(g.affine_select(out=before[:], in_=before[:], compare_op=ALU.is_ge, fill=1.0, base=0,
                                 pattern=[[-1, P]], channel_multiplier=1))
            g.memset(ones[:], 1.0)
            g.memset(ones16[:], 1.0)
            g.iota(iota_row[:], [[1, P]], base=0, channel_multiplier=0, allow_small_or_imprecise_dtypes=True)
            g.iota(iota_e[:], [[1, E]], base=-E, channel_multiplier=0, allow_small_or_imprecise_dtypes=True)
            g.iota(choice_id[:], [[1, K], [K * P, NT]], base=1, channel_multiplier=K,
                   allow_small_or_imprecise_dtypes=True)
            g.iota(pad_row[:], [[P, NA]], base=K * N + 1, channel_multiplier=1,
                   allow_small_or_imprecise_dtypes=True)
            link(g.memset(scan_keep[:], 1.0))
            g.memset(scan_keep[:, :, 0:1], 0.0).then_inc(s_const, 1)
            pool.wait_ge(s_q, 16 * 6)
            LQ = [[0, -1, -2, -3], [1, 0, -3, 2], [2, 3, 0, -1], [3, -2, 1, 0]]
            RQ = [[0, 1, 2, 3], [-1, 0, -3, 2], [-2, 3, 0, -1], [-3, -2, 1, 0]]
            for table, first, signs in ((lq, 4, LQ), (rq, 0, RQ)):
                for i in range(4):
                    for j in range(4):
                        q = signs[i][j]
                        last = g.tensor_scalar(table[:, i, j:j + 1], qsrc[:, first + abs(q):first + abs(q) + 1],
                                               -1.0 if q < 0 else 1.0, None, ALU.mult)
            last.then_inc(s_lr, 1)
            pool.wait_ge(s_xm, 1)
            g.partition_all_reduce(xmax[:, 1:2], xmax[:, 0:1], P, RMAX).then_inc(s_xa, 1)
            for b in range(NB):
                pool.wait_ge(s_ohe, b + 1)
                k, t = divmod(b * OB, NT)
                g.tensor_tensor(oha[:, b % 2], oha[:, b % 2],
                                choice_id[:, k, t:t + OB].unsqueeze(2).to_broadcast([P, OB, NA]),
                                ALU.mult).then_inc(s_oh, 1)

            def gather(a):
                for h in range(H):
                    at = src[:, 1, a * H + h:a * H + h + 1]
                    g.indirect_dma_start(out=gx[:, a % 2, h, :], out_offset=None, in_=x,
                                         in_offset=bass.IndirectOffsetOnAxis(ap=at, axis=0)).then_inc(s_g[a % 2], 16)

            def scatter(a):
                pool.wait_ge(s_ys, a + 1)
                for h in range(H):
                    at = dst[:, a * H + h:a * H + h + 1]
                    g.indirect_dma_start(out=ybuf, out_offset=bass.IndirectOffsetOnAxis(ap=at, axis=0),
                                         in_=ysb[:, a % 2, h, :], in_offset=None).then_inc(s_sc[a % 2], 16)

            pool.wait_ge(s_idx, 1)
            gather(0)
            gather(1)
            for a in range(NTILE):
                if a + 2 < NTILE:
                    pool.wait_ge(s_tp, a + 1)
                    gather(a + 2)
                if a:
                    scatter(a - 1)
            scatter(NTILE - 1)

            def add_bias(i, slot, j):
                pool.wait_ge(s_yi[slot], (j + 1) * 32)
                if later(i, SL):
                    pool.wait_ge(s_o, i - (SL - 1))
                g.tensor_tensor(xb[:, slot], xfin[:, slot], boutb[:].unsqueeze(1).to_broadcast([P, CT, D]),
                                ALU.add).then_inc(s_xb, 1)

            combine(pool, add_bias)

        @block.scalar
        def _(act):
            s = nc.scalar
            act.wait_ge(s_n2, 1)
            s.activation(nrm[:, 1, :], nrm[:, 0, :], ACT.Sqrt).then_inc(s_root, 1)

            def x_squares(g):
                act.wait_ge(s_x[g % 2], 16 * (g // 2 + 1))
                if g:
                    act.wait_ge(s_xsq, g)
                s.activation(xj[:], xin[:, g % 2].rearrange("p t d -> p (t d)"), ACT.Square,
                             accum_out=xss[:, g:g + 1]).then_inc(s_xsq, 1)

            def w1_squares(e):
                act.wait_ge(s_w1[e % 2], 16 * (e // 2 + 1))
                if e:
                    act.wait_ge(s_sq2, e)
                s.activation(junk[:], raw1[:, e % 2].rearrange("p k f -> p (k f)"), ACT.Square,
                             accum_out=wss[:, e, 0:1]).then_inc(s_sq1, 1)

            def w2_squares(e):
                act.wait_ge(s_w2[e % 2], 16 * (e // 2 + 1))
                act.wait_ge(s_sq1, e + 1)
                s.activation(junk[:], raw2[:, e % 2].rearrange("p k f -> p (k f)"), ACT.Square,
                             accum_out=wss[:, e, 1:2]).then_inc(s_sq2, 1)

            def piece(e, i):
                if i == 0:
                    act.wait_ge(s_s, e + 1)
                act.wait_ge(s_fp, 4 * e + i + 1)
                s.activation(w1s[:, e, 0, i // 2, (i % 2) * HF:(i % 2 + 1) * HF], FB[i % 2][:], ACT.Copy,
                             scale=s12[:, e, 0:1].bitcast(f32)).then_inc(s_fh, 1)
                if i == 1 and e + 1 < E:
                    w1_squares(e + 1)
                if i == 2 and e + 1 < E:
                    w2_squares(e + 1)
                if i == 3:
                    s.activation(w2s[:, e, 0].rearrange("p k d -> p (k d)"),
                                 raw2[:, e % 2].rearrange("p k d -> p (k d)"), ACT.Copy,
                                 scale=s12[:, e, 1:2].bitcast(f32)).then_inc(s_w2h, 1)

            x_squares(0)
            act.wait_ge(s_we, 1)
            s.activation(junk[:, 0:KD * D], wefft[:].rearrange("p k d -> p (k d)"), ACT.Square,
                         accum_out=oss[:, 0:1]).then_inc(s_wsq, 1)
            act.wait_ge(s_wsq, 1)
            w1_squares(0)
            w2_squares(0)
            for g in range(NG):
                if g + 1 < NG:
                    x_squares(g + 1)
                for i in range(2):
                    piece(g // 2, 2 * (g % 2) + i)
            piece(4, 0)
            act.wait_ge(s_ml, 1)
            s.activation(lg[:], t3[:], ACT.Exp).then_inc(s_exp, 1)
            for i in range(1, 4):
                piece(4, i)
            for b in range(NB):
                piece(5 + b // 4, b % 4)
            for i in range(4):
                piece(7, i)

            act.wait_ge(s_tab, 1)

            def rows_high(a, par):
                act.wait_ge(s_tp, a + 1)
                s.activation(xs[:, par, 0].rearrange("p k t -> p (k t)"), XB[par][:], ACT.Copy,
                             scale=sx[:, 0:1].bitcast(f32)).then_inc(s_xh, 1)

            def tile(a, par, j):
                e = act.value_load(tile_e[0:1, bass.ds(a, 1)], min_val=0, max_val=E - 1)
                for b in range(4):
                    act.wait_ge(s_mp, a * 4 + (b + 1))
                    if later(a, 1):
                        act.wait_ge(s_mq, a * 4 + (b - 3))
                    for c in range(2):
                        m = s.activation(midf[:, b, c * TS:(c + 1) * TS], FB[b][:, c * TS:(c + 1) * TS], ACT.Relu,
                                         bias=b1p[:, bass.ds(e, 1), 2 * b + c:2 * b + c + 1].rearrange("p e c -> p (e c)"),
                                         scale=cbits[:, 0, 1, bass.ds(e, 1)].bitcast(f32))
                    m.then_inc(s_mf, 1)
                if not isinstance(a, int) or a < NTILE - 1:
                    rows_high(a + 1, 1 - par)

            rows_high(0, 0)
            tiles(act, tile)

            def copy_mix(i, par):
                act.wait_ge(s_zp, i + 1)
                if later(i, 2):
                    act.wait_ge(s_op, i - 1)
                s.activation(zt[:, par].rearrange("p t k c -> p (t k c)"), bank[par][:], ACT.Copy).then_inc(s_zt, 1)

            def scale_first(i, slot, j):
                act.wait_ge(s_yi[slot], (j + 1) * 32)
                if later(i, 2):
                    act.wait_ge(s_z, i - 1)
                for t in range(CT):
                    m = s.activation(y1r[:, slot % 2, t, :], yin[:, slot, t, 0, :], ACT.Copy,
                                     scale=route[:, 0, bass.ds(i * CT + t, 1)])
                m.then_inc(s_y1, 1)
                if later(i, 1):
                    copy_mix(i - 1, (slot + 1) % 2)

            combine(act, scale_first)
            copy_mix(NS - 1, (NS - 1) % 2)

        @block.vector
        def _(dve):
            v = nc.vector
            chain = [0]

            def link(ins):
                chain[0] += 1
                ins.then_inc(s_dc, 1)
                dve.wait_ge(s_dc, chain[0])

            def bc(ap, shape):
                return ap.to_broadcast(shape)

            dve.wait_ge(s_q, 16 * 6)
            link(v.tensor_tensor(qsq[:, 0:4 + NCOND], qsrc[:, 0:4 + NCOND], qsrc[:, 0:4 + NCOND], ALU.mult))
            v.tensor_reduce(nrm[:, 2, 0:1], qsq[:, 0:4], AX.X, ALU.add)
            link(v.tensor_reduce(nrm[:, 2, 1:2], qsq[:, 4:4 + NCOND], AX.X, ALU.add))
            v.tensor_scalar(nrm[:, 0, :], nrm[:, 2, :], 1e-8, None, ALU.add).then_inc(s_n2, 1)
            dve.wait_ge(s_lr, 1)
            for m in range(4):
                to = coef if m == 0 else ctmp
                link(v.tensor_tensor(to[:], bc(lq[:, :, m:m + 1], [P, 4, 4]), bc(rq[:, m:m + 1, :], [P, 4, 4]),
                                     ALU.mult))
                if m:
                    link(v.tensor_tensor(coef[:], coef[:], ctmp[:], ALU.add))
            dve.wait_ge(s_root, 1)
            link(v.reciprocal(nrm[:, 3, :], nrm[:, 1, :]))
            link(v.tensor_tensor(nrm[:, 4, :], nrm[:, 3, :], nrm[:, 0, :], ALU.mult))
            link(v.tensor_tensor(nrm[:, 5, :], nrm[:, 4, :], nrm[:, 1, :], ALU.add))
            link(v.tensor_scalar(nrm[:, 6, :], nrm[:, 5, :], 0.5, None, ALU.mult))
            link(v.reciprocal(nrm[:, 7, :], nrm[:, 6, :]))
            link(v.tensor_tensor(qsq[:, 12:13], nrm[:, 7, 0:1], nrm[:, 7, 1:2], ALU.mult))
            link(v.tensor_tensor(qsq[:, 13:14], qsq[:, 12:13], qsrc[:, 4 + NCOND:5 + NCOND], ALU.mult))
            link(v.tensor_scalar(coef[:], coef[:], qsq[:, 13:14], None, ALU.mult))
            dve.wait_ge(s_const, 1)
            for k in range(KD):
                for half in range(2):
                    rows = slice(half * CH, (half + 1) * CH)
                    for ci in range(4):
                        last = v.tensor_scalar(rt[rows, k, ci * CH:(ci + 1) * CH], mask[rows, :],
                                               coef[rows, 2 * k + half, ci:ci + 1], None, ALU.mult)
            last.then_inc(s_rt, 1)
            dve.wait_ge(s_btp, 1)
            v.tensor_copy(bT[:], bank[4][:, 0:E * KF + KD]).then_inc(s_bt, 1)
            dve.wait_ge(s_wep, 1)
            v.tensor_copy(wefft[:].rearrange("p k d -> p (k d)"), bank[5][:]).then_inc(s_we, 1)
            dve.wait_ge(s_bt, 1)
            v.tensor_copy(binrep[:], bc(bT[:, E * KF:E * KF + KD].unsqueeze(2), [P, KD, P])).then_inc(s_rep, 1)
            dve.wait_ge(s_wgp, 1)
            v.tensor_copy(wg[:].rearrange("p k e -> p (k e)"), bank[3][:, 0:KD * E])
            v.tensor_copy(bg[:], bank[3][:, 64:64 + E]).then_inc(s_wg, 1)
            link(v.memset(fw2[:, 1:2], 1.0))
            dve.wait_ge(s_wnp, 1)
            v.tensor_copy(fw2[:, 0:1], bank[2][:, 0:1]).then_inc(s_wn, 1)
            dve.wait_ge(s_wn, 1)

            def x_pair(i):
                dve.wait_ge(s_xtp, i + 1)
                if i >= 2:
                    dve.wait_ge(s_lgp, i - 1)
                v.tensor_copy(xt_sb[:, i % 2].rearrange("p t k c -> p (t k c)"), bank[4 + i % 2][:]).then_inc(s_xt, 1)

            def powers(e):
                dve.wait_ge(s_sp, e + 1)
                link(v.tensor_tensor(sq[:, e], bank[2][:, 2 * e + 2:2 * e + 4], fw2[:], ALU.mult))
                link(v.tensor_scalar(hw[:, e], sq[:, e].bitcast(i32), 24, None, ALU.logical_shift_right))
                link(v.tensor_scalar(hk[:, e], hw[:, e], -1.0, 204.0, ALU.mult, ALU.add))
                v.tensor_scalar(s12[:, e], hk[:, e], 23, None, ALU.logical_shift_left).then_inc(s_s, 1)
                dve.wait_ge(s_s, e + 1)

            def piece(e, i):
                if i == 0:
                    powers(e)
                dve.wait_ge(s_fh, 4 * e + i + 1)
                q = slice((i % 2) * HF, (i % 2 + 1) * HF)
                v.scalar_tensor_tensor(w1s[:, e, 1, i // 2, q], FB[i % 2][:], s12[:, e, 0:1].bitcast(f32),
                                       w1s[:, e, 0, i // 2, q], ALU.mult, ALU.subtract).then_inc(s_fl, 1)
                if i == 3:
                    dve.wait_ge(s_w2h, e + 1)
                    v.scalar_tensor_tensor(w2s[:, e, 1].rearrange("p k d -> p (k d)"),
                                           raw2[:, e % 2].rearrange("p k d -> p (k d)"),
                                           s12[:, e, 1:2].bitcast(f32),
                                           w2s[:, e, 0].rearrange("p k d -> p (k d)"),
                                           ALU.mult, ALU.subtract).then_inc(s_w2l, 1)

            for g in range(NG):
                for i in range(2):
                    x_pair(2 * g + i)
                for i in range(2):
                    piece(g // 2, 2 * (g % 2) + i)
            T3 = [P, NT, E]

            def col(i):
                return mx[:, i, :]

            def wide(i):
                return bc(mx[:, i, :].unsqueeze(2), T3)

            def ie():
                return bc(iota_e[:].unsqueeze(1), T3)

            dve.wait_ge(s_xsq, NG)
            v.tensor_reduce(xmax[:, 0:1], xss[:], AX.X, ALU.max).then_inc(s_xm, 1)
            dve.wait_ge(s_lgp, NT // 2)
            dve.wait_ge(s_wg, 1)
            link(v.tensor_tensor(lg[:], bank[6][:, 0:NT * E].rearrange("p (t e) -> p t e", t=NT),
                                 bc(bg[:].unsqueeze(1), T3), ALU.add))
            link(v.tensor_reduce(col(0), lg[:], AX.X, ALU.max))
            v.tensor_tensor(t3[:], lg[:], wide(0), ALU.subtract).then_inc(s_ml, 1)
            piece(4, 0)
            dve.wait_ge(s_exp, 1)
            link(v.tensor_reduce(col(1), lg[:], AX.X, ALU.add))
            link(v.reciprocal(col(2), col(1)))
            link(v.tensor_tensor(pr[:], lg[:], wide(2), ALU.mult))
            for k in range(K):
                link(v.tensor_reduce(col(3 + k), pr[:], AX.X, ALU.max))
                link(v.tensor_tensor(t3[:], pr[:], wide(3 + k), ALU.is_equal))
                link(v.tensor_tensor(t3[:], t3[:], ie(), ALU.mult))
                link(v.tensor_reduce(col(5), t3[:], AX.X, ALU.min))
                link(v.tensor_tensor(oh[:, k], ie(), wide(5), ALU.is_equal))
                if k == 0:
                    link(v.scalar_tensor_tensor(pr[:], oh[:, 0], -2.0, pr[:], ALU.mult, ALU.add))
            v.tensor_tensor(m16[:].rearrange("p e t -> p t e"), oh[:, 0], oh[:, 1], ALU.add).then_inc(s_m, 1)
            piece(4, 1)
            link(v.tensor_tensor(col(5), col(3), col(4), ALU.add))
            link(v.reciprocal(col(6), col(5)))
            link(v.tensor_tensor(route[:], mx[:, 3:5, :], bc(mx[:, 6:7, :], [P, K, NT]), ALU.mult))
            dve.wait_ge(s_rank, 1)
            rk = bank[4][:].rearrange("p (s e t) -> p s e t", s=2, e=E)
            link(v.tensor_copy(tot[:], rk[:, 1]))
            link(v.tensor_tensor_scan(incl[:].rearrange("p e t -> p (e t)"), scan_keep[:].rearrange("p e t -> p (e t)"),
                                      tot[:].rearrange("p e t -> p (e t)"), 0.0, ALU.mult, ALU.add))
            link(v.tensor_scalar(cnti[:, 0, :], incl[:, :, NT - 1], float(TS - 1), None, ALU.add))
            link(v.tensor_scalar(cnti[:, 1, :], cnti[:, 0, :], TS.bit_length() - 1, None, ALU.logical_shift_right))
            link(v.tensor_copy(cnt[:, 0, :], cnti[:, 1, :]))
            link(v.tensor_tensor_scan(cnt[:, 1, :], ones[:, 0:E], cnt[:, 0, :], 0.0, ALU.mult, ALU.add))
            link(v.tensor_tensor(cnt[:, 2, :], cnt[:, 1, :], cnt[:, 0, :], ALU.subtract))
            link(v.tensor_scalar(cnt[:, 3, :], cnt[:, 2, :], float(TS), None, ALU.mult))
            link(v.tensor_tensor(sv[:], incl[:], tot[:], ALU.subtract))
            link(v.tensor_tensor(sv[:], sv[:], rk[:, 0], ALU.add))
            link(v.tensor_tensor(sv[:], sv[:], bc(cnt[:, 3, :].unsqueeze(2), [P, E, NT]), ALU.add))
            for k in range(K):
                link(v.tensor_tensor(t3[:], oh[:, k], sv[:].rearrange("p e t -> p t e"), ALU.mult))
                link(v.tensor_reduce(slot[:, k, :], t3[:], AX.X, ALU.add))
            piece(4, 2)
            link(v.tensor_copy(sloti[:, 0], slot[:]))
            link(v.tensor_scalar(sloti[:, 1], sloti[:, 0], P.bit_length() - 1, None, ALU.logical_shift_right))
            link(v.tensor_scalar(sloti[:, 2], sloti[:, 0], P - 1, None, ALU.bitwise_and))
            link(v.tensor_copy(slotab[:], sloti[:, 1:3]))
            piece(4, 3)
            for b in range(NB):
                k, t = divmod(b * OB, NT)
                if b >= 2:
                    dve.wait_ge(s_ohp, b - 1)
                v.tensor_tensor(oha[:, b % 2], iota_row[:, 0:NA].unsqueeze(1).to_broadcast([P, OB, NA]),
                                slotab[:, 0, k, t:t + OB].unsqueeze(2).to_broadcast([P, OB, NA]),
                                ALU.is_equal).then_inc(s_ohe, 1)
                v.tensor_tensor(ohb[:, b % 2], iota_row[:].unsqueeze(1).to_broadcast([P, OB, P]),
                                slotab[:, 1, k, t:t + OB].unsqueeze(2).to_broadcast([P, OB, P]),
                                ALU.is_equal).then_inc(s_ohu, 1)
                piece(5 + b // 4, b % 4)
            link(v.tensor_tensor(te[:, 0], bc(iota_row[0:1, 0:NTILE].unsqueeze(2), [1, NTILE, E]),
                                 bc(cnt[0:1, 1, :].unsqueeze(1), [1, NTILE, E]), ALU.is_ge))
            link(v.tensor_reduce(te[:, 1, :, 0], te[:, 0], AX.X, ALU.add))
            link(v.tensor_scalar(tile_e[:], te[:, 1, :, 0], float(E - 1), None, ALU.min))
            dve.wait_ge(s_ohp, NB)
            dmap = bank[7][:, 0:NA]
            link(v.scalar_tensor_tensor(ptmp[:], dmap, 0.0, pad_row[:], ALU.is_equal, ALU.mult))
            link(v.scalar_tensor_tensor(dst[:], dmap, -1.0, ptmp[:], ALU.add, ALU.add))
            link(v.tensor_scalar(src[:, 0, :], dmap, -1.0, 0.0, ALU.add, ALU.max))
            v.tensor_scalar(src[:, 1, :], src[:, 0, :], K.bit_length() - 1, None,
                            ALU.logical_shift_right).then_inc(s_idx, 1)

            for i in range(4):
                piece(7, i)
            dve.wait_ge(s_b1p, E)
            link(v.tensor_tensor(b1p[:].rearrange("p e c -> p (e c)"), bank[3][:, 0:E * KF], bT[:, 0:E * KF], ALU.add))
            link(v.tensor_tensor(b1sq[:], b1p[:], b1p[:], ALU.mult))
            v.tensor_reduce(oss[:, 1:1 + E], b1sq[:], AX.X, ALU.add).then_inc(s_bsq, 1)
            dve.wait_ge(s_xa, 1)
            v.tensor_copy(sqo[:, 0:1], xmax[:, 1:2])
            dve.wait_ge(s_bsp, 1)
            link(v.tensor_copy(sqo[:, 1:1 + E], bank[2][:, 32:32 + E]))
            link(v.tensor_scalar(ho[:], sqo[:].bitcast(i32), 24, None, ALU.logical_shift_right))
            link(v.tensor_scalar(sx[:, 1:2], ho[:, 0:1], -1.0, 204.0, ALU.mult, ALU.add))
            link(v.tensor_scalar(sx[:, 0:1], sx[:, 1:2], 23, None, ALU.logical_shift_left))
            link(v.tensor_copy(hf[:, 0, 0:1 + E], ho[:]))
            link(v.tensor_copy(hf[:, 1, 0:2 * E], hw[:].rearrange("p e q -> p (e q)")))
            hx, hb = hf[:, 0, 0:1], hf[:, 0, 1:1 + E]
            h12 = hf[:, 1, 0:2 * E].rearrange("p (e q) -> p q e", q=2)
            link(v.tensor_scalar(kk[:, 0, :], h12[:, 0, :], hx, -62.0, ALU.add, ALU.add))
            link(v.tensor_tensor(kk[:, 1, :], kk[:, 0, :], hb, ALU.max))
            link(v.tensor_scalar(kk[:, 2, :], kk[:, 1, :], -1.0, 76.0, ALU.mult, ALU.add))
            link(v.tensor_tensor(kk[:, 3, :], kk[:, 2, :], h12[:, 0, :], ALU.add))
            link(v.tensor_scalar(kk[:, 3, :], kk[:, 3, :], hx, 127.0 - 154.0, ALU.add, ALU.add))
            link(v.tensor_tensor(kk[:, 4, :], h12[:, 1, :], kk[:, 2, :], ALU.subtract))
            link(v.tensor_scalar(kk[:, 4, :], kk[:, 4, :], 127.0 - 77.0, None, ALU.add))
            link(v.tensor_scalar(kk[:, 5, :], kk[:, 2, :], 127.0, None, ALU.add))
            link(v.tensor_scalar(cbits[:, :, 0, :], kk[:, 3:6, :], 1.0, 254.0, ALU.max, ALU.min))
            link(v.tensor_scalar(cbits[:, :, 1, :], cbits[:, :, 0, :], 23, None, ALU.logical_shift_left))
            dve.wait_ge(s_fl, 4 * E)
            dve.wait_ge(s_w2l, E)
            dve.wait_ge(s_late, 16 * 3)
            v.tensor_tensor(b1p[:], b1p[:], bc(cbits[:, 2, 1, :].bitcast(f32).unsqueeze(2), [P, E, KF]),
                            ALU.mult).then_inc(s_tab, 1)

            def rows_low(a, par):
                dve.wait_ge(s_xh, a + 1)
                v.scalar_tensor_tensor(xs[:, par, 1].rearrange("p k t -> p (k t)"), XB[par][:],
                                       sx[:, 0:1].bitcast(f32), xs[:, par, 0].rearrange("p k t -> p (k t)"),
                                       ALU.mult, ALU.subtract).then_inc(s_xl, 1)

            def y_out(a, par, before):
                e = dve.value_load(tile_e[0:1, bass.ds(a, 1)], min_val=0, max_val=E - 1)
                dve.wait_ge(s_yp, a + 1)
                if later(a, 2):
                    dve.wait_ge(s_sc[par], before * (16 * H))
                for h in range(H):
                    last = v.scalar_tensor_tensor(ysb[:, par, h, :], YB[par][:, h * D:(h + 1) * D],
                                                  cbits[:, 1, 1, bass.ds(e, 1)].bitcast(f32),
                                                  b2b[:, bass.ds(e, 1), :].rearrange("p e d -> p (e d)"),
                                                  ALU.mult, ALU.add)
                last.then_inc(s_ys, 1)

            def tile(a, par, j):
                for b in range(4):
                    dve.wait_ge(s_mf, a * 4 + (b + 1))
                    v.tensor_copy(mids[:, par, 0, b, :], midf[:, b, :]).then_inc(s_mh, 1)
                    dve.wait_ge(s_mh, a * 4 + (b + 1))
                    v.tensor_tensor(mids[:, par, 1, b, :], midf[:, b, :], mids[:, par, 0, b, :],
                                    ALU.subtract).then_inc(s_mq, 1)
                if not isinstance(a, int) or a < NTILE - 1:
                    rows_low(a + 1, 1 - par)
                if later(a, 1):
                    y_out(a - 1, 1 - par, j if par else j - 1)

            rows_low(0, 0)
            tiles(dve, tile)
            y_out(NTILE - 1, 0, NTILE // 2)

            def finish(i, slot, j):
                dve.wait_ge(s_op, i + 1)
                dve.wait_ge(s_xb, i + 1)
                if later(i, SL):
                    dve.wait_ge(s_st[slot], j * 16)
                v.tensor_tensor(osb[:, slot].rearrange("p t d -> p (t d)"), bank[2 + slot % 2][:],
                                xb[:, slot].rearrange("p t d -> p (t d)"), ALU.add).then_inc(s_o, 1)

            def mix(i, slot, j):
                dve.wait_ge(s_yi[slot], (j + 1) * 32)
                dve.wait_ge(s_y1, i + 1)
                if later(i, 2):
                    dve.wait_ge(s_zp, i - 1)
                for t in range(CT):
                    last = v.scalar_tensor_tensor(ztok[:, slot % 2, t, :], yin[:, slot, t, 1, :],
                                                  route[:, 1, bass.ds(i * CT + t, 1)], y1r[:, slot % 2, t, :],
                                                  ALU.mult, ALU.add)
                last.then_inc(s_z, 1)
                if later(i, 1):
                    finish(i - 1, (slot - 1) % SL, j if slot else j - 1)

            combine(dve, mix)
            finish(NS - 1, SL - 1, NS // SL - 1)

        @block.tensor
        def _(pe):
            mm, tr = nc.tensor.matmul, nc.tensor.transpose
            NR = E * KF + KD
            pe.wait_ge(s_const, 1)
            pe.wait_ge(s_small, 16 * 4)
            tr(bank[4][:, 0:NR], brow[:], ident[0:NR, 0:NR]).then_inc(s_btp, 1)
            pe.wait_ge(s_rt, 1)
            pe.wait_ge(s_win, 16)
            for kd in range(KD):
                for kj in range(KD):
                    last = mm(bank[5][:, kd * D:(kd + 1) * D], winr[:, kj, kd * P:(kd + 1) * P], rt[:, kj, :],
                              start=(kj == 0), stop=(kj == KD - 1))
            last.then_inc(s_wep, 1)
            pe.wait_ge(s_we, 1)
            for ki in range(KD):
                for kd in range(KD):
                    mm(bank[3][:, ki * E:(ki + 1) * E], wefft[:, kd, ki * P:(ki + 1) * P], wgr[:, kd, :],
                       start=(kd == 0), stop=(kd == KD - 1))
            pe.wait_ge(s_rep, 1)
            for kd in range(KD):
                mm(bank[3][:, 64:64 + E], binrep[:, kd, :], wgr[:, kd, :], start=(kd == 0), stop=False)
            mm(bank[3][:, 64:64 + E], ones[0:1, :], bgr[:], start=False, stop=True).then_inc(s_wgp, 1)
            pe.wait_ge(s_wsq, 1)
            mm(bank[2][:, 0:1], ones[:], oss[:, 0:1], start=True, stop=True).then_inc(s_wnp, 1)
            pe.wait_ge(s_wg, 1)

            def logits(i):
                pe.wait_ge(s_xt, i + 1)
                for t in range(2):
                    for k in range(KD):
                        last = mm(bank[6][:, (2 * i + t) * E:(2 * i + t + 1) * E], xt_sb[:, i % 2, t, k, :],
                                  wg[:, k, :], start=(k == 0), stop=(k == KD - 1))
                last.then_inc(s_lgp, 1)

            def x_pair(i):
                g = 2 * i // XG
                pe.wait_ge(s_x[g % 2], 16 * (g // 2 + 1))
                if i >= 2:
                    pe.wait_ge(s_xt, i - 1)
                for t in range(2):
                    for k in range(KD):
                        last = tr(bank[4 + i % 2][:, (t * KD + k) * P:(t * KD + k + 1) * P],
                                  xin[:, g % 2, (2 * i + t) % XG, k * P:(k + 1) * P], ident[:])
                last.then_inc(s_xtp, 1)

            def piece(e, i):
                if i == 0:
                    pe.wait_ge(s_sq2, e + 1)
                    pe.wait_ge(s_wn if e == 0 else s_s, max(e, 1))
                    mm(bank[2][:, 2 * e + 2:2 * e + 4], ones[:], wss[:, e], start=True, stop=True).then_inc(s_sp, 1)
                    pe.wait_ge(s_w1[e % 2], 16 * (e // 2 + 1))
                if 4 * e + i >= 2:
                    pe.wait_ge(s_fl, 4 * e + i - 1)
                for kd in range(KD):
                    last = mm(FB[i % 2][:], wefft[:, kd, (i // 2) * P:(i // 2 + 1) * P],
                              raw1[:, e % 2, kd, (i % 2) * HF:(i % 2 + 1) * HF], start=(kd == 0), stop=(kd == KD - 1))
                last.then_inc(s_fp, 1)
                if i == 3:
                    for c in range(KF):
                        for kd in range(KD):
                            last = mm(bank[3][:, e * KF + c:e * KF + c + 1], raw1[:, e % 2, kd, c * P:(c + 1) * P],
                                      bT[:, E * KF + kd:E * KF + kd + 1], start=(kd == 0), stop=(kd == KD - 1))
                    last.then_inc(s_b1p, 1)

            for g in range(NG):
                x_pair(2 * g)
                if g:
                    logits(2 * g - 1)
                x_pair(2 * g + 1)
                logits(2 * g)
                for i in range(2):
                    piece(g // 2, 2 * (g % 2) + i)
            logits(2 * NG - 1)
            piece(4, 0)
            piece(4, 1)
            pe.wait_ge(s_m, 1)
            m_et = m16[:].rearrange("p e t -> p (e t)")
            mm(bank[4][:, 0:E * NT], before[:], m_et, start=True, stop=True)
            mm(bank[4][:, E * NT:2 * E * NT], ones16[:], m_et, start=True, stop=True).then_inc(s_rank, 1)
            piece(4, 2)
            piece(4, 3)
            for b in range(NB):
                piece(5 + b // 4, b % 4)
                pe.wait_ge(s_oh, b + 1)
                pe.wait_ge(s_ohu, b + 1)
                for q in range(OB):
                    last = mm(bank[7][:, 0:NA], ohb[:, b % 2, q, :], oha[:, b % 2, q, :],
                              start=(b == 0 and q == 0), stop=(b == NB - 1 and q == OB - 1))
                last.then_inc(s_ohp, 1)
            for i in range(4):
                piece(7, i)
            pe.wait_ge(s_bsq, 1)
            pe.wait_ge(s_s, E)
            mm(bank[2][:, 32:32 + E], ones[:], oss[:, 1:1 + E], start=True, stop=True).then_inc(s_bsp, 1)
            pe.wait_ge(s_tab, 1)

            def rows_t(a, par, j):
                pe.wait_ge(s_g[par], (j + 1) * (16 * H))
                if later(a, 2):
                    pe.wait_ge(s_xl, a - 1)
                for k in range(KD):
                    for h in range(H):
                        last = tr(XB[par][:, k * TS + h * P:k * TS + (h + 1) * P], gx[:, par, h, k * P:(k + 1) * P],
                                  ident[:])
                last.then_inc(s_tp, 1)

            def w1_at(e, l, k, c):
                return w1s[:, bass.ds(e, 1), l, k, c * P:(c + 1) * P].rearrange("p e f -> p (e f)")

            def w2_at(e, l, c):
                return w2s[:, bass.ds(e, 1), l, c, :].rearrange("p e f -> p (e f)")

            def first_layer(a, par, e):
                pe.wait_ge(s_xl, a + 1)
                for b in range(4):
                    if later(a, 1):
                        pe.wait_ge(s_mf, a * 4 + (b - 3))
                    for c in range(2):
                        o = FB[b][:, c * TS:(c + 1) * TS]
                        for k in range(KD):
                            w = w1_at(e, 0, k, 2 * b + c)
                            mm(o, w, xs[:, par, 0, k, :], start=(k == 0), stop=False)
                            mm(o, w, xs[:, par, 1, k, :], start=False, stop=False)
                            last = mm(o, w1_at(e, 1, k, 2 * b + c), xs[:, par, 0, k, :], start=False,
                                      stop=(k == KD - 1))
                    last.then_inc(s_mp, 1)

            def second_layer(a, par, e):
                if later(a, 2):
                    pe.wait_ge(s_ys, a - 1)
                for b in range(4):
                    pe.wait_ge(s_mq, a * 4 + (b + 1))
                    for c in range(2):
                        f = 2 * b + c
                        for l, w in ((0, 0), (1, 0), (0, 1)):
                            for h in range(H):
                                last = mm(YB[par][:, h * D:(h + 1) * D],
                                          mids[:, par, l, b, c * TS + h * P:c * TS + (h + 1) * P], w2_at(e, w, f),
                                          start=(f == 0 and l == 0 and w == 0 and h == 0),
                                          stop=(f == KF - 1 and w == 1), skip_group_check=True)
                last.then_inc(s_yp, 1)

            def expert(a):
                return pe.value_load(tile_e[0:1, bass.ds(a, 1)], min_val=0, max_val=E - 1)

            def tile(a, par, j):
                first_layer(a, par, expert(a))
                if not isinstance(a, int) or a < NTILE - 1:
                    rows_t(a + 1, 1 - par, j + par)
                if later(a, 1):
                    second_layer(a - 1, 1 - par, expert(a - 1))

            rows_t(0, 0, 0)
            tiles(pe, tile)
            second_layer(NTILE - 1, 0, expert(NTILE - 1))

            def project(i, par):
                pe.wait_ge(s_zt, i + 1)
                if later(i, 2):
                    pe.wait_ge(s_o, i - 1)
                for t in range(CT):
                    for k in range(KD):
                        last = mm(bank[2 + par][:, t * D:(t + 1) * D], zt[:, par, t, k, :], wout[:, k, :],
                                  start=(k == 0), stop=(k == KD - 1))
                last.then_inc(s_op, 1)

            def mix_t(i, slot, j):
                pe.wait_ge(s_z, i + 1)
                if later(i, 2):
                    pe.wait_ge(s_zt, i - 1)
                for t in range(CT):
                    for k in range(KD):
                        last = tr(bank[slot % 2][:, (t * KD + k) * P:(t * KD + k + 1) * P],
                                  ztok[:, slot % 2, t, k * P:(k + 1) * P], ident[:])
                last.then_inc(s_zp, 1)
                if later(i, 1):
                    project(i - 1, (slot + 1) % 2)

            combine(pe, mix_t)
            project(NS - 1, (NS - 1) % 2)


_ARGS = ['x', 'cond_256', 'L0_cond_q_right', 'L0_cond_spectral_gate', 'L0_ffn_W_in', 'L0_ffn_b_in', 'L0_ffn_W_gate',
         'L0_ffn_b_gate', 'L0_ffn_W1', 'L0_ffn_b1', 'L0_ffn_W2', 'L0_ffn_b2', 'L0_ffn_W_out', 'L0_ffn_b_out']


def kernel(**inputs):
    import numpy as _np
    import concourse.bacc as _bacc
    from concourse import mybir as _mybir
    from concourse.bass_utils import run_bass_kernel_spmd as _run

    nc = _bacc.Bacc("TRN2", target_bir_lowering=False, num_devices=1)
    arrays, args = {}, []
    for name in _ARGS:
        a = _np.ascontiguousarray(inputs[name])
        if name == 'x':
            a = a.reshape(-1, a.shape[-1])
        if name == 'L0_cond_spectral_gate':
            a = a.reshape(1, -1)
        arrays[f"in_{name}"] = a
        args.append(nc.dram_tensor(f"in_{name}", a.shape, _mybir.dt.from_np(a.dtype), kind="ExternalInput").ap())
    shape = _np.shape(inputs['x'])
    out = nc.dram_tensor("out_0", (shape[0] * shape[1], shape[2]), _mybir.dt.float32, kind="ExternalOutput").ap()
    moe_program(nc, *args, out)
    r = _run(nc, [arrays], core_ids=[0])
    return r.results[0]["out_0"].reshape(shape)
```

```python
import concourse.bass as bass
from concourse import mybir
from contextlib import ExitStack

RMAX = bass.bass_isa.ReduceOp.max


def moe_program(nc, x, cond, q_right, gate, W_in, b_in, W_gate, b_gate, W1, b1, W2, b2, W_out, b_out, out):
    f32, f16, i32 = mybir.dt.float32, mybir.dt.float16, mybir.dt.int32
    ALU, ACT, AX = mybir.AluOpType, mybir.ActivationFunctionType, mybir.AxisListType
    P = 128
    N, D = x.shape
    E, _, F = W1.shape
    KD, KF = D // P, F // P
    NT = N // P
    K = 2
    TS = 256
    H = TS // P
    NTILE = (K * N + E * (TS - 1)) // TS
    NA = NTILE * H
    CH = D // 4
    NCOND = cond.shape[0]
    EP = 5
    XG = 4
    OB = 8

    zbuf = nc.dram_tensor("z_by_token", (N, D), f32, kind="Internal").ap()
    ybuf = nc.dram_tensor("y_by_choice", (K * N + NTILE * TS, D), f32, kind="Internal").ap()

    ctx = ExitStack()
    with ctx:
        def sb(name, shape, dt):
            return ctx.enter_context(nc.sbuf_tensor(name, shape, dt))

        def sem(name):
            return ctx.enter_context(nc.semaphore(name))

        bank = [ctx.enter_context(nc.psum_tensor(f"bank{i}", [P, 512], f32)) for i in range(8)]

        FB = [bank[i] for i in (0, 1, 6, 7)]
        XB = [bank[i] for i in (2, 3)]
        YB = [bank[i] for i in (4, 5)]

        w1s = sb("w1s", [P, E, 2, KD, F], f16)
        w2s = sb("w2s", [P, E, 2, KF, D], f16)
        ident = sb("ident", [P, P], f32)
        ones = sb("ones", [P, P], f32)
        ones16 = sb("ones16", [P, P], f16)
        before = sb("before", [P, P], f16)
        mask = sb("mask", [P, CH], f32)
        iota_row = sb("iota_row", [P, P], f32)
        iota_e = sb("iota_e", [P, E], f32)
        choice_id = sb("choice_id", [P, 2, K, NT], f32)
        pad_row = sb("pad_row", [P, NA], f32)
        scan_keep = sb("scan_keep", [P, E, NT], f32)
        qsrc = sb("qsrc", [P, 4 + NCOND + 1], f32)
        winr = sb("winr", [P, KD, D], f32)
        wgr = sb("wgr", [P, KD, E], f32)
        brow = sb("brow", [E * KF + KD, P], f32)
        bgr = sb("bgr", [1, E], f32)
        b2b = sb("b2b", [P, E, D], f32)
        boutb = sb("boutb", [P, D], f32)
        wout = sb("wout", [P, KD, D], f32)
        lq = sb("lq", [P, 4, 4], f32)
        rq = sb("rq", [P, 4, 4], f32)
        coef = sb("coef", [P, 4, 4], f32)
        ctmp = sb("ctmp", [P, 4, 4], f32)
        nrm = sb("nrm", [P, 8, 2], f32)
        qsq = sb("qsq", [P, 16], f32)
        binb = sb("binb", [P, D], f32)
        wg = sb("wg", [P, KD, E], f32)
        bT = sb("bT", [P, E * KF + KD], f32)
        bg = sb("bg", [P, E], f32)
        last1 = w1s[:, E - 1].bitcast(f32).rearrange("p l k f -> p (l k f)")
        last2 = w2s[:, E - 1].bitcast(f32).rearrange("p l k f -> p (l k f)")
        lg, pr, t3 = (last2[:, i * NT * E:(i + 1) * NT * E].rearrange("p (t e) -> p t e", t=NT) for i in range(3))
        oh = last2[:, 3 * NT * E:5 * NT * E].rearrange("p (k t e) -> p k t e", k=K, t=NT)
        tot, incl, sv = (last2[:, i * NT * E:(i + 1) * NT * E].rearrange("p (e t) -> p e t", e=E) for i in (5, 6, 7))
        last16 = w1s[:, E - 1].rearrange("p l k f -> p (l k f)")
        ohb = last16[:, 0:2 * OB * P].rearrange("p (s i c) -> p s i c", s=2, i=OB)
        ohc = last16[:, 2 * OB * P:2 * OB * (P + NA)].rearrange("p (s i c) -> p s i c", s=2, i=OB)
        oha = sb("oha", [P, 2, OB, 2, NA], f16)
        rt = last1[:, 0:KD * D].rearrange("p (k d) -> p k d", k=KD)
        binrep = last1[:, 512:512 + KD * P].rearrange("p (k d) -> p k d", k=KD)
        xt_sb = last1[:, 1024:2048].rearrange("p (s t k c) -> p s t k c", s=2, t=2, k=KD)
        weff, wefft = (last2[:, i * KD * D:(i + 1) * KD * D].rearrange("p (k d) -> p k d", k=KD) for i in range(2))
        m16 = sb("m16", [P, E, NT], f16)
        mx = sb("mx", [P, 8, NT], f32)
        route = sb("route", [P, K, NT], f32)
        cnt = sb("cnt", [P, 6, E], f32)
        cnti = sb("cnti", [P, 2, E], i32)
        slot = sb("slot", [P, K, NT], f32)
        sloti = sb("sloti", [P, 3, K, NT], i32)
        slotab = sb("slotab", [P, 2, K, NT], f32)
        ptmp = sb("ptmp", [P, NA], f32)
        dmap = sb("dmap", [P, NA], f32)
        dst = sb("dst", [P, NA], i32)
        src = sb("src", [P, 2, NA], i32)
        tile_e = sb("tile_e", [1, NTILE], i32)
        te = sb("te", [1, 2, NTILE, E], f32)
        zss = sb("zss", [P, NT // 2], f32)
        zmax = sb("zmax", [P, 2], f32)
        wss = sb("wss", [P, E, 2], f32)
        bss = sb("bss", [P, E], f32)
        sq = sb("sq", [P, E, 2], f32)
        hw = sb("hw", [P, E, 2], i32)
        hk = sb("hk", [P, E, 2], i32)
        s12 = sb("s12", [P, E, 2], i32)
        sqo = sb("sqo", [P, 1 + E], f32)
        ho = sb("ho", [P, 1 + E], i32)
        sx = sb("sx", [P, 2], i32)
        hf = sb("hf", [P, 3, 1 + 2 * E], f32)
        kk = sb("kk", [P, 6, E], f32)
        cbits = sb("cbits", [P, 3, 2, E], i32)
        b1p = sb("b1p", [P, E, KF], f32)
        b1sq = sb("b1sq", [P, E, KF], f32)
        junk = sb("junk", [P, 2048], f16)
        zst = w1s[:, E - 2].bitcast(f32).rearrange("p l k f -> p (l k f)").rearrange("p (s c) -> p s c", s=4)
        zj = w2s[:, E - 2, 0].rearrange("p k d -> p (k d)")[:, 0:2 * D]
        RAW = KD * F
        region = sb("region", [P, 4 * RAW + 2 * XG * D], f32)
        raw1 = region[:, 0:2 * RAW].rearrange("p (s k f) -> p s k f", s=2, k=KD)
        raw2 = region[:, 2 * RAW:4 * RAW].rearrange("p (s k f) -> p s k f", s=2, k=KF)
        xin = region[:, 4 * RAW:4 * RAW + 2 * XG * D].rearrange("p (s t d) -> p s t d", s=2, t=XG)

        gx = region[:, 4 * RAW:4 * RAW + 2 * H * D].rearrange("p (s h d) -> p s h d", s=2, h=H)
        ysb = region[:, 4 * RAW + 2 * H * D:4 * RAW + 4 * H * D].rearrange("p (s h d) -> p s h d", s=2, h=H)
        midf = region[:, 0:KF * TS].rearrange("p (b c) -> p b c", b=4)
        xs = region[:, KF * TS:(KF + 2 * KD) * TS].bitcast(f16).rearrange("p (s l k t) -> p s l k t", s=2, l=2, k=KD)
        mids = region[:, (KF + 2 * KD) * TS:(3 * KF + 2 * KD) * TS].bitcast(f16).rearrange(
            "p (s l b c) -> p s l b c", s=2, l=2, b=4)
        CT = 2
        NS = NT // CT
        SL = 4
        fin = w1s[:].bitcast(f32).rearrange("p e l k f -> p (e l k f)")

        def fin_cut(at, n, pattern, **sizes):
            return fin[:, at * D:(at + n) * D].rearrange(pattern, **sizes)

        xall = fin_cut(0, NT, "p (t d) -> p t d", t=NT)
        yin = fin_cut(NT, SL * CT * K, "p (s t k d) -> p s t k d", s=SL, t=CT, k=K)
        ztok, y1r = (fin_cut(NT + SL * CT * K + i * 2 * CT, 2 * CT, "p (s t d) -> p s t d", s=2, t=CT)
                     for i in range(2))
        zt = fin_cut(NT + SL * CT * K + 4 * CT, 2 * CT, "p (s t k c) -> p s t k c", s=2, t=CT, k=KD)

        s_q, s_win, s_small, s_late = sem("q_loaded"), sem("win_loaded"), sem("small_loaded"), sem("late_loaded")
        s_x = [sem(f"x_loaded{i}") for i in range(2)]
        s_w1 = [sem(f"w1_loaded{i}") for i in range(2)]
        s_w2 = [sem(f"w2_loaded{i}") for i in range(2)]
        s_const = sem("constants_ready")
        s_pc = sem("pool_chain")
        s_lr = sem("quaternion_tables_ready")
        s_dc = sem("dve_chain")
        s_rep = sem("bias_replicas_ready")
        s_n2 = sem("norm_squares_ready")
        s_root = sem("norm_roots_ready")
        s_rt = sem("rotation_ready")
        s_btp = sem("biases_transposed")
        s_bt = sem("biases_copied")
        s_wep = sem("weff_product")
        s_we = sem("weff_copied")
        s_wgp = sem("gate_product")
        s_wg = sem("gate_copied")
        s_xtp = sem("x_transposed")
        s_xt = sem("xt_copied")
        s_zpr, s_zc, s_zsq = sem("z_and_logits_product"), sem("z_copied"), sem("z_squared")
        s_zst = [sem(f"z_stored{i}") for i in range(4)]
        s_ml = sem("logits_less_max")
        s_exp = sem("exp_ready")
        s_m = sem("choices_ready")
        s_rank = sem("ranks_product")
        s_ohe = sem("column_onehots_compared")
        s_oh = sem("column_onehots_times_id")
        s_ohu = sem("row_onehots_compared")
        s_ohp = sem("onehots_multiplied")
        s_te = sem("tile_experts_ready")
        s_idx = sem("slot_map_ready")
        s_zn = sem("z_norm_ready")
        s_zm = sem("z_norm_max_ready")
        s_sq1, s_sq2 = sem("w1_squared"), sem("w2_squared")
        s_sp, s_s = sem("norms_product"), sem("powers_ready")
        s_wh, s_wl = sem("weights_high"), sem("weights_low")
        s_ws, s_wp = sem("pool_weights_scaled"), sem("pool_weights_low")
        s_bsq = sem("b1_squared")
        s_ho = sem("exponents_ready")
        s_tab = sem("tables_ready")
        s_g = [sem(f"rows_gathered{i}") for i in range(2)]
        s_tp = sem("rows_transposed")
        s_xh, s_xl = sem("rows_high"), sem("rows_low")
        s_mp = sem("mid_product")
        s_mf = sem("mid_relu")
        s_mh, s_mq = sem("mid_high"), sem("mid_split")
        s_yp, s_ys = sem("y_product"), sem("y_ready")
        s_sc = [sem(f"rows_scattered{i}") for i in range(2)]
        s_yi = [sem(f"pairs_loaded{i}") for i in range(SL)]
        s_y1 = sem("first_choice_scaled")
        s_z = sem("choices_mixed")
        s_zp = sem("mix_transposed")
        s_zt = sem("mix_copied")
        s_op = sem("out_product")
        s_xb = sem("x_plus_bias")
        s_o = sem("out_ready")
        s_xf = sem("residual_loaded")
        s_st = sem("out_stored")

        block = ctx.enter_context(nc.Block())

        x_t = x.rearrange("(t p) d -> p t d", p=P)
        out_t = out.rearrange("(t p) d -> p t d", p=P)
        z_t = zbuf.rearrange("(t p) d -> p t d", p=P)
        y_t = ybuf[0:K * N, :].rearrange("(t p k) d -> p t k d", p=P, k=K)
        NG = NT // XG
        NB = NT * K // OB

        def quarter(e, i):
            if i < 2:
                return raw1[:, e % 2, i, :], w1s[:, e, 0, i, :], w1s[:, e, 1, i, :], s12[:, e, 0:1].bitcast(f32)
            k = slice((i - 2) * KF // 2, (i - 1) * KF // 2)
            return tuple(a.rearrange("p k d -> p (k d)") for a in (raw2[:, e % 2, k], w2s[:, e, 0, k], w2s[:, e, 1, k])
                         ) + (s12[:, e, 1:2].bitcast(f32),)

        def wait_low(eng, e, n):
            if e == EP:
                eng.wait_ge(s_wp, n)
            else:
                eng.wait_ge(s_wl, 4 * (e - (e > EP)) + n)

        def later(i, n):
            return not isinstance(i, int) or i >= n

        def tiles(eng, step):
            for a in range(4):
                step(a, a % 2, a // 2)
            with eng.Fori(2, NTILE // 2) as j:
                step(j * 2, 0, j)
                step(j * 2 + 1, 1, j)
            step(NTILE - 1, 0, NTILE // 2)

        def combine(eng, step):
            for i in range(SL):
                step(i, i, 0)
            with eng.Fori(1, NS // SL) as j:
                for q in range(SL):
                    step(j * SL + q, q, j)

        @block.sync
        def _(sp):
            for half in range(2):
                rows = slice(half * CH, (half + 1) * CH)
                with nc.allow_non_contiguous_dma(reason="a few hundred words, one per channel"):
                    sp.dma_start(qsrc[rows, 0:4], q_right.rearrange("c q -> q c")).then_inc(s_q, 16)
                    sp.dma_start(qsrc[rows, 4:4 + NCOND], cond.rearrange("c q -> q c")).then_inc(s_q, 16)
                    sp.dma_start(qsrc[rows, 4 + NCOND:5 + NCOND], gate.rearrange("c q -> q c")).then_inc(s_q, 16)
            sp.dma_start(raw1[:, 0], W1[0].rearrange("(k p) f -> p k f", p=P)).then_inc(s_w1[0], 16)
            sp.dma_start(winr[:], W_in.rearrange("(k p) n -> p k n", p=P)).then_inc(s_win, 16)
            sp.dma_start(binb[:], b_in.partition_broadcast(P)).then_inc(s_win, 16)
            sp.dma_start(wgr[:], W_gate.rearrange("(k p) n -> p k n", p=P)).then_inc(s_small, 16)
            sp.dma_start(brow[0:E * KF, :], b1.rearrange("e (c p) -> (e c) p", p=P)).then_inc(s_small, 16)
            sp.dma_start(brow[E * KF:E * KF + KD, :], b_in.rearrange("(k p) -> k p", p=P)).then_inc(s_small, 16)
            sp.dma_start(bgr[:], b_gate.rearrange("(a e) -> a e", a=1)).then_inc(s_small, 16)

            def load_x(g):
                if g >= 2:
                    sp.wait_ge(s_xtp, XG // 2 * (g - 1))
                sp.dma_start(xin[:, g % 2], x_t[:, g * XG:(g + 1) * XG, :]).then_inc(s_x[g % 2], 16)

            def load_w1(e):
                if e >= 2:
                    wait_low(sp, e - 2, 2)
                    sp.wait_ge(s_sq1, e - 1)
                sp.dma_start(raw1[:, e % 2], W1[e].rearrange("(k p) f -> p k f", p=P)).then_inc(s_w1[e % 2], 16)

            def load_w2(e):
                if e >= 2:
                    sp.wait_ge(s_sq2, e - 1)
                    wait_low(sp, e - 2, 4)
                sp.dma_start(raw2[:, e % 2], W2[e].rearrange("(k p) f -> p k f", p=P)).then_inc(s_w2[e % 2], 16)

            load_w2(0)
            load_x(0)
            load_x(1)
            load_w1(1)
            load_w2(1)
            load_x(2)
            load_w1(2)
            load_w2(2)
            load_x(3)
            for g in range(4, NG):
                if g % 2 == 0:
                    load_w1(g // 2 + 1)
                    load_w2(g // 2 + 1)
                load_x(g)
            for e in range(NG // 2 + 1, E):
                load_w1(e)
                load_w2(e)
            sp.dma_start(wout[:], W_out.rearrange("(k p) n -> p k n", p=P)).then_inc(s_late, 16)
            sp.dma_start(b2b[:].rearrange("p e d -> p (e d)"),
                         b2.rearrange("e d -> (e d)").partition_broadcast(P)).then_inc(s_late, 16)
            sp.dma_start(boutb[:], b_out.partition_broadcast(P)).then_inc(s_late, 16)
            sp.wait_ge(s_mp, 4 * NTILE)
            for c in range(4):
                t = slice(c * NT // 4, (c + 1) * NT // 4)
                sp.dma_start(xall[:, t], x_t[:, t, :]).then_inc(s_xf, 16)
            sp.wait_ge(s_sc[0], 16 * H * ((NTILE + 1) // 2))
            sp.wait_ge(s_sc[1], 16 * H * (NTILE // 2))

            def load(i, slot):
                sp.wait_ge(s_z, i - (SL - 1))
                sp.dma_start(yin[:, slot], y_t[:, bass.ds(i * CT, CT)]).then_inc(s_yi[slot], 16)

            def store(i):
                sp.wait_ge(s_o, i + 1)
                sp.dma_start(out_t[:, bass.ds(i * CT, CT), :], xall[:, bass.ds(i * CT, CT)]).then_inc(s_st, 16)

            for i in range(SL):
                sp.dma_start(yin[:, i], y_t[:, i * CT:(i + 1) * CT]).then_inc(s_yi[i], 16)
            with sp.Fori(0, NS // SL - 1) as j:
                for q in range(SL):
                    load(j * SL + (q + SL), q)
                    store(j * SL + q)
            for i in range(NS - SL, NS):
                store(i)
            sp.wait_ge(s_st, 16 * NS)

        @block.gpsimd
        def _(pool):
            chain = [0]

            def link(ins):
                chain[0] += 1
                ins.then_inc(s_pc, 1)
                pool.wait_ge(s_pc, chain[0])

            g = nc.gpsimd
            link(g.memset(ident[:], 0.0))
            g.affine_select(out=ident[:], in_=ident[:], compare_op=ALU.not_equal, fill=1.0, base=0,
                            pattern=[[-1, P]], channel_multiplier=1)
            link(g.memset(mask[:], 0.0))
            link(g.affine_select(out=mask[:], in_=mask[:], compare_op=ALU.not_equal, fill=1.0, base=0,
                                 pattern=[[-1, CH]], channel_multiplier=1))
            link(g.affine_select(out=mask[:], in_=mask[:], compare_op=ALU.not_equal, fill=1.0, base=-CH,
                                 pattern=[[-1, CH]], channel_multiplier=1))
            link(g.memset(before[:], 0.0))
            link(g.affine_select(out=before[:], in_=before[:], compare_op=ALU.is_ge, fill=1.0, base=0,
                                 pattern=[[-1, P]], channel_multiplier=1))
            g.memset(ones[:], 1.0)
            g.memset(ones16[:], 1.0)
            g.iota(iota_row[:], [[1, P]], base=0, channel_multiplier=0, allow_small_or_imprecise_dtypes=True)
            g.iota(iota_e[:], [[1, E]], base=-E, channel_multiplier=0, allow_small_or_imprecise_dtypes=True)
            g.iota(choice_id[:, 0], [[0, K], [1, NT]], base=0, channel_multiplier=0,
                   allow_small_or_imprecise_dtypes=True)
            g.iota(choice_id[:, 1], [[1, K], [0, NT]], base=1, channel_multiplier=K,
                   allow_small_or_imprecise_dtypes=True)
            g.iota(pad_row[:], [[P, NA]], base=K * N + 1, channel_multiplier=1,
                   allow_small_or_imprecise_dtypes=True)
            link(g.memset(scan_keep[:], 1.0))
            g.memset(scan_keep[:, :, 0:1], 0.0).then_inc(s_const, 1)
            for i in range(NT // 2):
                pool.wait_ge(s_zc, i + 1)
                pool.dma_start(z_t[:, 2 * i:2 * i + 2, :], zst[:, i % 4].rearrange("p (t d) -> p t d", t=2)
                               ).then_inc(s_zst[i % 4], 16)
            pool.wait_ge(s_zn, 1)
            g.partition_all_reduce(zmax[:, 1:2], zmax[:, 0:1], P, RMAX).then_inc(s_zm, 1)
            for i in range(4):
                raw, high, low, _ = quarter(EP, i)
                pool.wait_ge(s_wh, 4 * EP + i + 1)
                g.tensor_tensor(low, raw, high, ALU.subtract).then_inc(s_wp, 1)
            for b in range(NB):
                pool.wait_ge(s_ohe, b + 1)
                if b >= 2:
                    pool.wait_ge(s_ohp, b - 1)
                k, t = divmod(b * OB, NT)
                for part in range(2):
                    last = g.tensor_tensor(oha[:, b % 2, :, part, :], ohc[:, b % 2],
                                           choice_id[:, part, k, t:t + OB].unsqueeze(2).to_broadcast([P, OB, NA]),
                                           ALU.mult)
                last.then_inc(s_oh, 1)
            pool.wait_ge(s_ho, 1)
            pool.wait_ge(s_s, E)
            link(g.tensor_copy(hf[:, 0, 0:1 + E], ho[:]))
            link(g.tensor_copy(hf[:, 1, 0:2 * E], hw[:].rearrange("p e q -> p (e q)")))
            hx, hb = hf[:, 0, 0:1], hf[:, 0, 1:1 + E]
            h12 = hf[:, 1, 0:2 * E].rearrange("p (e q) -> p q e", q=2)
            link(g.tensor_scalar(kk[:, 0, :], h12[:, 0, :], hx, -62.0, ALU.add, ALU.add))
            link(g.tensor_tensor(kk[:, 0, :], kk[:, 0, :], hb, ALU.subtract))
            link(g.tensor_scalar(kk[:, 0, :], kk[:, 0, :], 0.0, None, ALU.max))
            link(g.tensor_tensor(kk[:, 1, :], kk[:, 0, :], hb, ALU.add))
            link(g.tensor_scalar(kk[:, 2, :], kk[:, 1, :], -1.0, 76.0, ALU.mult, ALU.add))

            def gather(a):
                for h in range(H):
                    at = src[:, 1, a * H + h:a * H + h + 1]
                    g.indirect_dma_start(out=gx[:, a % 2, h, :], out_offset=None, in_=zbuf,
                                         in_offset=bass.IndirectOffsetOnAxis(ap=at, axis=0)).then_inc(s_g[a % 2], 16)

            def scatter(a):
                pool.wait_ge(s_ys, a + 1)
                for h in range(H):
                    at = dst[:, a * H + h:a * H + h + 1]
                    g.indirect_dma_start(out=ybuf, out_offset=bass.IndirectOffsetOnAxis(ap=at, axis=0),
                                         in_=ysb[:, a % 2, h, :], in_offset=None).then_inc(s_sc[a % 2], 16)

            pool.wait_ge(s_idx, 1)
            for q in range(4):
                pool.wait_ge(s_zst[q], 16 * (NT // 8))
            gather(0)
            link(g.tensor_tensor(kk[:, 3, :], kk[:, 2, :], h12[:, 0, :], ALU.add))
            link(g.tensor_scalar(kk[:, 3, :], kk[:, 3, :], hx, 127.0 - 154.0, ALU.add, ALU.add))
            link(g.tensor_tensor(kk[:, 4, :], h12[:, 1, :], kk[:, 2, :], ALU.subtract))
            link(g.tensor_scalar(kk[:, 4, :], kk[:, 4, :], 127.0 - 77.0, None, ALU.add))
            link(g.tensor_scalar(kk[:, 5, :], kk[:, 2, :], 127.0, None, ALU.add))
            link(g.tensor_scalar(cbits[:, :, 0, :], kk[:, 3:6, :], 1.0, 254.0, ALU.max, ALU.min))
            link(g.tensor_scalar(cbits[:, :, 1, :], cbits[:, :, 0, :], float(1 << 23), None, ALU.mult))
            pool.wait_ge(s_late, 16 * 3)
            g.tensor_tensor(b1p[:], bT[:, 0:E * KF].rearrange("p (e c) -> p e c", e=E),
                            cbits[:, 2, 1, :].bitcast(f32).unsqueeze(2).to_broadcast([P, E, KF]),
                            ALU.mult).then_inc(s_tab, 1)
            gather(1)
            for a in range(NTILE):
                if a + 2 < NTILE:
                    pool.wait_ge(s_tp, a + 1)
                    gather(a + 2)
                if a:
                    scatter(a - 1)
            scatter(NTILE - 1)

            def add_bias(i, slot, j):
                t = bass.ds(i * CT, CT)
                g.tensor_tensor(xall[:, t], xall[:, t], boutb[:].unsqueeze(1).to_broadcast([P, CT, D]),
                                ALU.add).then_inc(s_xb, 1)

            pool.wait_ge(s_xf, 16 * 4)
            combine(pool, add_bias)

        @block.scalar
        def _(act):
            s = nc.scalar
            act.wait_ge(s_n2, 1)
            s.activation(nrm[:, 1, :], nrm[:, 0, :], ACT.Sqrt).then_inc(s_root, 1)

            def z_squares(i):
                act.wait_ge(s_zc, i + 1)
                if i:
                    act.wait_ge(s_zsq, i)
                s.activation(zj[:], zst[:, i % 4], ACT.Square, accum_out=zss[:, i:i + 1]).then_inc(s_zsq, 1)

            def w1_squares(e):
                act.wait_ge(s_w1[e % 2], 16 * (e // 2 + 1))
                if e:
                    act.wait_ge(s_sq2, e)
                s.activation(junk[:], raw1[:, e % 2].rearrange("p k f -> p (k f)"), ACT.Square,
                             accum_out=wss[:, e, 0:1]).then_inc(s_sq1, 1)

            def w2_squares(e):
                act.wait_ge(s_w2[e % 2], 16 * (e // 2 + 1))
                act.wait_ge(s_sq1, e + 1)
                s.activation(junk[:], raw2[:, e % 2].rearrange("p k f -> p (k f)"), ACT.Square,
                             accum_out=wss[:, e, 1:2]).then_inc(s_sq2, 1)

            def piece(e, i):
                if i == 0:
                    act.wait_ge(s_s, e + 1)
                    if e == E - 2:
                        for q in range(4):
                            act.wait_ge(s_zst[q], 16 * (NT // 8))
                raw, high, _, scale = quarter(e, i)
                if e == EP:
                    s.activation(raw, raw, ACT.Copy, scale=scale).then_inc(s_ws, 1)
                    act.wait_ge(s_ws, i + 1)
                    s.activation(high, raw, ACT.Copy).then_inc(s_wh, 1)
                else:
                    s.activation(high, raw, ACT.Copy, scale=scale).then_inc(s_wh, 1)
                if i == 1 and e + 1 < E:
                    w1_squares(e + 1)
                if i == 2 and e + 1 < E:
                    w2_squares(e + 1)

            w1_squares(0)
            w2_squares(0)
            for i in range(4):
                piece(0, i)
            for i in range(NT // 2):
                piece(1 + i // 4, i % 4)
                if i:
                    z_squares(i - 1)
            z_squares(NT // 2 - 1)
            act.wait_ge(s_ml, 1)
            s.activation(lg[:], t3[:], ACT.Exp).then_inc(s_exp, 1)
            for e in range(5, E):
                for i in range(4):
                    if e == E - 1 and i == 0:
                        act.wait_ge(s_ohp, NB)
                    piece(e, i)

            act.wait_ge(s_te, 1)
            act.wait_ge(s_tab, 1)
            wait_low(act, E - 1, 2)

            def rows_high(a, par):
                act.wait_ge(s_tp, a + 1)
                s.activation(xs[:, par, 0].rearrange("p k t -> p (k t)"), XB[par][:], ACT.Copy,
                             scale=sx[:, 0:1].bitcast(f32)).then_inc(s_xh, 1)

            def tile(a, par, j):
                e = act.value_load(tile_e[0:1, bass.ds(a, 1)], min_val=0, max_val=E - 1)
                for b in range(4):
                    act.wait_ge(s_mp, a * 4 + (b + 1))
                    if later(a, 1):
                        act.wait_ge(s_mq, a * 4 + (b - 3))
                    for c in range(2):
                        f = 2 * b + c
                        m = s.activation(midf[:, b, c * TS:(c + 1) * TS], FB[b][:, c * TS:(c + 1) * TS], ACT.Relu,
                                         bias=b1p[:, bass.ds(e, 1), f:f + 1].rearrange("p e c -> p (e c)"),
                                         scale=cbits[:, 0, 1, bass.ds(e, 1)].bitcast(f32))
                    m.then_inc(s_mf, 1)
                if not isinstance(a, int) or a < NTILE - 1:
                    rows_high(a + 1, 1 - par)

            rows_high(0, 0)
            tiles(act, tile)

            def copy_mix(i, par):
                act.wait_ge(s_zp, i + 1)
                if later(i, 2):
                    act.wait_ge(s_op, i - 1)
                s.activation(zt[:, par].rearrange("p t k c -> p (t k c)"), bank[par][:], ACT.Copy).then_inc(s_zt, 1)

            def scale_first(i, slot, j):
                act.wait_ge(s_yi[slot], (j + 1) * 16)
                if later(i, 2):
                    act.wait_ge(s_z, i - 1)
                for t in range(CT):
                    m = s.activation(y1r[:, slot % 2, t, :], yin[:, slot, t, 0, :], ACT.Copy,
                                     scale=route[:, 0, bass.ds(i * CT + t, 1)])
                m.then_inc(s_y1, 1)
                if later(i, 1):
                    copy_mix(i - 1, (slot + 1) % 2)

            combine(act, scale_first)
            copy_mix(NS - 1, (NS - 1) % 2)

        @block.vector
        def _(dve):
            v = nc.vector
            chain = [0]

            def link(ins):
                chain[0] += 1
                ins.then_inc(s_dc, 1)
                dve.wait_ge(s_dc, chain[0])

            def bc(ap, shape):
                return ap.to_broadcast(shape)

            dve.wait_ge(s_q, 16 * 6)
            link(v.tensor_tensor(qsq[:, 0:4 + NCOND], qsrc[:, 0:4 + NCOND], qsrc[:, 0:4 + NCOND], ALU.mult))
            v.tensor_reduce(nrm[:, 2, 0:1], qsq[:, 0:4], AX.X, ALU.add)
            link(v.tensor_reduce(nrm[:, 2, 1:2], qsq[:, 4:4 + NCOND], AX.X, ALU.add))
            v.tensor_scalar(nrm[:, 0, :], nrm[:, 2, :], 1e-8, None, ALU.add).then_inc(s_n2, 1)
            LQ = [[0, -1, -2, -3], [1, 0, -3, 2], [2, 3, 0, -1], [3, -2, 1, 0]]
            RQ = [[0, 1, 2, 3], [-1, 0, -3, 2], [-2, 3, 0, -1], [-3, -2, 1, 0]]
            for table, first, signs in ((lq, 4, LQ), (rq, 0, RQ)):
                for i in range(4):
                    for j in range(4):
                        q = signs[i][j]
                        last = v.tensor_scalar(table[:, i, j:j + 1], qsrc[:, first + abs(q):first + abs(q) + 1],
                                               -1.0 if q < 0 else 1.0, None, ALU.mult)
            last.then_inc(s_lr, 1)
            dve.wait_ge(s_lr, 1)
            for m in range(4):
                to = coef if m == 0 else ctmp
                link(v.tensor_tensor(to[:], bc(lq[:, :, m:m + 1], [P, 4, 4]), bc(rq[:, m:m + 1, :], [P, 4, 4]),
                                     ALU.mult))
                if m:
                    link(v.tensor_tensor(coef[:], coef[:], ctmp[:], ALU.add))
            dve.wait_ge(s_root, 1)
            link(v.reciprocal(nrm[:, 3, :], nrm[:, 1, :]))
            link(v.tensor_tensor(nrm[:, 4, :], nrm[:, 3, :], nrm[:, 0, :], ALU.mult))
            link(v.tensor_tensor(nrm[:, 5, :], nrm[:, 4, :], nrm[:, 1, :], ALU.add))
            link(v.tensor_scalar(nrm[:, 6, :], nrm[:, 5, :], 0.5, None, ALU.mult))
            link(v.reciprocal(nrm[:, 7, :], nrm[:, 6, :]))
            link(v.tensor_tensor(qsq[:, 12:13], nrm[:, 7, 0:1], nrm[:, 7, 1:2], ALU.mult))
            link(v.tensor_tensor(qsq[:, 13:14], qsq[:, 12:13], qsrc[:, 4 + NCOND:5 + NCOND], ALU.mult))
            link(v.tensor_scalar(coef[:], coef[:], qsq[:, 13:14], None, ALU.mult))
            dve.wait_ge(s_const, 1)
            for half in range(2):
                rows = slice(half * CH, (half + 1) * CH)
                for k in range(KD):
                    last = v.tensor_tensor(rt[rows, k, :].rearrange("p (i c) -> p i c", i=4),
                                           bc(mask[rows, :].unsqueeze(1), [CH, 4, CH]),
                                           bc(coef[rows, 2 * k + half, :].unsqueeze(2), [CH, 4, CH]), ALU.mult)
            last.then_inc(s_rt, 1)
            dve.wait_ge(s_btp, 1)
            v.tensor_copy(bT[:], bank[7][:, 0:E * KF + KD]).then_inc(s_bt, 1)
            dve.wait_ge(s_bt, 1)
            v.tensor_copy(binrep[:], bc(bT[:, E * KF:E * KF + KD].unsqueeze(2), [P, KD, P])).then_inc(s_rep, 1)

            def x_pair(i):
                dve.wait_ge(s_xtp, i + 1)
                if i >= 2:
                    dve.wait_ge(s_zpr, i - 1)
                v.tensor_copy(xt_sb[:, i % 2].rearrange("p t k c -> p (t k c)"), bank[4 + i % 2][:]).then_inc(s_xt, 1)

            def z_pair(i):
                dve.wait_ge(s_zpr, i + 1)
                if i >= 4:
                    dve.wait_ge(s_zst[i % 4], 16 * (i // 4))
                    dve.wait_ge(s_zsq, i - 3)
                v.tensor_tensor(zst[:, i % 4].rearrange("p (t d) -> p t d", t=2),
                                bank[i % 2][:].rearrange("p (t d) -> p t d", t=2),
                                bc(binb[:].unsqueeze(1), [P, 2, D]), ALU.add).then_inc(s_zc, 1)

            def powers(e):
                dve.wait_ge(s_sp, e + 1)
                link(v.tensor_copy(sq[:, e], bank[2][:, 2 * e:2 * e + 2]))
                link(v.tensor_scalar(hw[:, e], sq[:, e].bitcast(i32), 24, None, ALU.logical_shift_right))
                link(v.tensor_scalar(hk[:, e], hw[:, e], -1.0, 204.0, ALU.mult, ALU.add))
                v.tensor_scalar(s12[:, e], hk[:, e], 23, None, ALU.logical_shift_left).then_inc(s_s, 1)
                dve.wait_ge(s_s, e + 1)

            def piece(e, i):
                raw, high, low, scale = quarter(e, i)
                dve.wait_ge(s_wh, 4 * e + i + 1)
                v.scalar_tensor_tensor(low, raw, scale, high, ALU.mult, ALU.subtract).then_inc(s_wl, 1)

            link(v.tensor_tensor(b1sq[:].rearrange("p e c -> p (e c)"), bT[:, 0:E * KF], bT[:, 0:E * KF], ALU.mult))
            v.tensor_reduce(bss[:], b1sq[:], AX.X, ALU.add).then_inc(s_bsq, 1)
            x_pair(0)
            x_pair(1)
            dve.wait_ge(s_sp, 1)
            v.tensor_copy(sqo[:, 1:1 + E], bank[2][:, 32:32 + E])
            powers(0)
            piece(0, 0)
            piece(0, 1)
            dve.wait_ge(s_wep, 1)
            v.tensor_copy(weff.rearrange("p k d -> p (k d)"), bank[1][:])
            v.tensor_copy(wefft.rearrange("p k d -> p (k d)"), bank[6][:]).then_inc(s_we, 1)
            piece(0, 2)
            dve.wait_ge(s_wgp, 1)
            v.tensor_copy(wg[:].rearrange("p k e -> p (k e)"), bank[3][:, 0:KD * E])
            v.tensor_copy(bg[:], bank[3][:, 64:64 + E]).then_inc(s_wg, 1)
            piece(0, 3)
            powers(1)
            for i in range(NT // 2):
                if 1 <= i < NT // 2 - 1:
                    x_pair(i + 1)
                piece(1 + i // 4, i % 4)
                z_pair(i)
                if i % 4 == 3:
                    powers(2 + i // 4)
            T3 = [P, NT, E]

            def col(i):
                return mx[:, i, :]

            def wide(i):
                return bc(mx[:, i, :].unsqueeze(2), T3)

            def ie():
                return bc(iota_e[:].unsqueeze(1), T3)

            dve.wait_ge(s_zpr, NT // 2)
            dve.wait_ge(s_wg, 1)
            link(v.tensor_tensor(lg[:], bank[6][:, 0:NT * E].rearrange("p (t e) -> p t e", t=NT),
                                 bc(bg[:].unsqueeze(1), T3), ALU.add))
            link(v.tensor_reduce(col(0), lg[:], AX.X, ALU.max))
            v.tensor_tensor(t3[:], lg[:], wide(0), ALU.subtract).then_inc(s_ml, 1)
            dve.wait_ge(s_zsq, NT // 2)
            v.tensor_reduce(zmax[:, 0:1], zss[:], AX.X, ALU.max).then_inc(s_zn, 1)
            dve.wait_ge(s_exp, 1)
            link(v.tensor_reduce(col(1), lg[:], AX.X, ALU.add))
            link(v.reciprocal(col(2), col(1)))
            link(v.tensor_tensor(pr[:], lg[:], wide(2), ALU.mult))
            for k in range(K):
                link(v.tensor_reduce(col(3 + k), pr[:], AX.X, ALU.max))
                link(v.tensor_tensor(t3[:], pr[:], wide(3 + k), ALU.is_equal))
                link(v.tensor_tensor(t3[:], t3[:], ie(), ALU.mult))
                link(v.tensor_reduce(col(5), t3[:], AX.X, ALU.min))
                link(v.tensor_tensor(oh[:, k], ie(), wide(5), ALU.is_equal))
                if k == 0:
                    link(v.scalar_tensor_tensor(pr[:], oh[:, 0], -2.0, pr[:], ALU.mult, ALU.add))
            v.tensor_tensor(m16[:].rearrange("p e t -> p t e"), oh[:, 0], oh[:, 1], ALU.add).then_inc(s_m, 1)
            link(v.tensor_tensor(col(5), col(3), col(4), ALU.add))
            link(v.reciprocal(col(6), col(5)))
            link(v.tensor_tensor(route[:], mx[:, 3:5, :], bc(mx[:, 6:7, :], [P, K, NT]), ALU.mult))
            dve.wait_ge(s_rank, 1)
            rk = bank[4][:].rearrange("p (s e t) -> p s e t", s=2, e=E)
            link(v.tensor_copy(tot[:], rk[:, 1]))
            link(v.tensor_tensor_scan(incl[:].rearrange("p e t -> p (e t)"), scan_keep[:].rearrange("p e t -> p (e t)"),
                                      tot[:].rearrange("p e t -> p (e t)"), 0.0, ALU.mult, ALU.add))
            link(v.tensor_scalar(cnti[:, 0, :], incl[:, :, NT - 1], float(TS - 1), None, ALU.add))
            link(v.tensor_scalar(cnti[:, 1, :], cnti[:, 0, :], TS.bit_length() - 1, None, ALU.logical_shift_right))
            link(v.tensor_copy(cnt[:, 0, :], cnti[:, 1, :]))
            link(v.tensor_tensor_scan(cnt[:, 1, :], ones[:, 0:E], cnt[:, 0, :], 0.0, ALU.mult, ALU.add))
            link(v.tensor_tensor(cnt[:, 2, :], cnt[:, 1, :], cnt[:, 0, :], ALU.subtract))
            link(v.tensor_scalar(cnt[:, 3, :], cnt[:, 2, :], float(TS), None, ALU.mult))
            link(v.tensor_tensor(sv[:], incl[:], tot[:], ALU.subtract))
            link(v.tensor_tensor(sv[:], sv[:], rk[:, 0], ALU.add))
            link(v.tensor_tensor(sv[:], sv[:], bc(cnt[:, 3, :].unsqueeze(2), [P, E, NT]), ALU.add))
            for k in range(K):
                link(v.tensor_tensor(t3[:], oh[:, k], sv[:].rearrange("p e t -> p t e"), ALU.mult))
                link(v.tensor_reduce(slot[:, k, :], t3[:], AX.X, ALU.add))
            link(v.tensor_copy(sloti[:, 0], slot[:]))
            link(v.tensor_scalar(sloti[:, 1], sloti[:, 0], P.bit_length() - 1, None, ALU.logical_shift_right))
            link(v.tensor_scalar(sloti[:, 2], sloti[:, 0], P - 1, None, ALU.bitwise_and))
            link(v.tensor_copy(slotab[:], sloti[:, 1:3]))
            powers(6)
            dve.wait_ge(s_zm, 1)
            link(v.tensor_copy(sqo[:, 0:1], zmax[:, 1:2]))
            link(v.tensor_scalar(ho[:], sqo[:].bitcast(i32), 24, None, ALU.logical_shift_right))
            link(v.tensor_scalar(sx[:, 1:2], ho[:, 0:1], -1.0, 204.0, ALU.mult, ALU.add))
            v.tensor_scalar(sx[:, 0:1], sx[:, 1:2], 23, None, ALU.logical_shift_left).then_inc(s_ho, 1)
            for b in range(NB):
                k, t = divmod(b * OB, NT)
                if b >= 2:
                    dve.wait_ge(s_oh, b - 1)
                    dve.wait_ge(s_ohp, b - 1)
                v.tensor_tensor(ohc[:, b % 2], iota_row[:, 0:NA].unsqueeze(1).to_broadcast([P, OB, NA]),
                                slotab[:, 0, k, t:t + OB].unsqueeze(2).to_broadcast([P, OB, NA]),
                                ALU.is_equal).then_inc(s_ohe, 1)
                v.tensor_tensor(ohb[:, b % 2], iota_row[:].unsqueeze(1).to_broadcast([P, OB, P]),
                                slotab[:, 1, k, t:t + OB].unsqueeze(2).to_broadcast([P, OB, P]),
                                ALU.is_equal).then_inc(s_ohu, 1)
                if b % 2:
                    piece(6, b // 2)
                if b == NB - 2:
                    powers(7)
            dve.wait_ge(s_ohp, NB)
            link(v.tensor_copy(ptmp[:], bank[7][:, NA:2 * NA]))
            link(v.scalar_tensor_tensor(dmap[:], bank[7][:, 0:NA], float(K * P), ptmp[:], ALU.mult, ALU.add))
            link(v.scalar_tensor_tensor(ptmp[:], dmap[:], 0.0, pad_row[:], ALU.is_equal, ALU.mult))
            link(v.scalar_tensor_tensor(dst[:], dmap[:], -1.0, ptmp[:], ALU.add, ALU.add))
            link(v.tensor_scalar(src[:, 0, :], dmap[:], -1.0, 0.0, ALU.add, ALU.max))
            v.tensor_scalar(src[:, 1, :], src[:, 0, :], K.bit_length() - 1, None,
                            ALU.logical_shift_right).then_inc(s_idx, 1)
            link(v.tensor_tensor(te[:, 0], bc(iota_row[0:1, 0:NTILE].unsqueeze(2), [1, NTILE, E]),
                                 bc(cnt[0:1, 1, :].unsqueeze(1), [1, NTILE, E]), ALU.is_ge))
            link(v.tensor_reduce(te[:, 1, :, 0], te[:, 0], AX.X, ALU.add))
            v.tensor_scalar(tile_e[:], te[:, 1, :, 0], float(E - 1), None, ALU.min).then_inc(s_te, 1)

            for i in range(4):
                piece(7, i)
            def rows_low(a, par):
                dve.wait_ge(s_xh, a + 1)
                v.scalar_tensor_tensor(xs[:, par, 1].rearrange("p k t -> p (k t)"), XB[par][:],
                                       sx[:, 0:1].bitcast(f32), xs[:, par, 0].rearrange("p k t -> p (k t)"),
                                       ALU.mult, ALU.subtract).then_inc(s_xl, 1)

            def y_out(a, par, before):
                e = dve.value_load(tile_e[0:1, bass.ds(a, 1)], min_val=0, max_val=E - 1)
                dve.wait_ge(s_yp, a + 1)
                if later(a, 2):
                    dve.wait_ge(s_sc[par], before * (16 * H))
                for h in range(H):
                    last = v.scalar_tensor_tensor(ysb[:, par, h, :], YB[par][:, h * D:(h + 1) * D],
                                                  cbits[:, 1, 1, bass.ds(e, 1)].bitcast(f32),
                                                  b2b[:, bass.ds(e, 1), :].rearrange("p e d -> p (e d)"),
                                                  ALU.mult, ALU.add)
                last.then_inc(s_ys, 1)

            def tile(a, par, j):
                for b in range(4):
                    dve.wait_ge(s_mf, a * 4 + (b + 1))
                    v.tensor_copy(mids[:, par, 0, b, :], midf[:, b, :]).then_inc(s_mh, 1)
                    dve.wait_ge(s_mh, a * 4 + (b + 1))
                    v.tensor_tensor(mids[:, par, 1, b, :], midf[:, b, :], mids[:, par, 0, b, :],
                                    ALU.subtract).then_inc(s_mq, 1)
                if not isinstance(a, int) or a < NTILE - 1:
                    rows_low(a + 1, 1 - par)
                if later(a, 1):
                    y_out(a - 1, 1 - par, j if par else j - 1)

            dve.wait_ge(s_te, 1)
            rows_low(0, 0)
            dve.wait_ge(s_tab, 1)
            tiles(dve, tile)
            y_out(NTILE - 1, 0, NTILE // 2)

            def finish(i, par):
                dve.wait_ge(s_op, i + 1)
                dve.wait_ge(s_xb, i + 1)
                t = bass.ds(i * CT, CT)
                v.tensor_tensor(xall[:, t], bank[2 + par][:].rearrange("p (t d) -> p t d", t=CT), xall[:, t],
                                ALU.add).then_inc(s_o, 1)

            def mix(i, slot, j):
                dve.wait_ge(s_yi[slot], (j + 1) * 16)
                dve.wait_ge(s_y1, i + 1)
                if later(i, 2):
                    dve.wait_ge(s_zp, i - 1)
                for t in range(CT):
                    last = v.scalar_tensor_tensor(ztok[:, slot % 2, t, :], yin[:, slot, t, 1, :],
                                                  route[:, 1, bass.ds(i * CT + t, 1)], y1r[:, slot % 2, t, :],
                                                  ALU.mult, ALU.add)
                last.then_inc(s_z, 1)
                if later(i, 2):
                    finish(i - 2, slot % 2)

            combine(dve, mix)
            finish(NS - 2, 0)
            finish(NS - 1, 1)

        @block.tensor
        def _(pe):
            mm, tr = nc.tensor.matmul, nc.tensor.transpose
            NR = E * KF + KD
            pe.wait_ge(s_const, 1)
            pe.wait_ge(s_small, 16 * 4)
            tr(bank[7][:, 0:NR], brow[:], ident[0:NR, 0:NR]).then_inc(s_btp, 1)

            def x_pair(i):
                g = 2 * i // XG
                pe.wait_ge(s_x[g % 2], 16 * (g // 2 + 1))
                if i >= 2:
                    pe.wait_ge(s_xt, i - 1)
                for t in range(2):
                    for k in range(KD):
                        last = tr(bank[4 + i % 2][:, (t * KD + k) * P:(t * KD + k + 1) * P],
                                  xin[:, g % 2, (2 * i + t) % XG, k * P:(k + 1) * P], ident[:])
                last.then_inc(s_xtp, 1)

            def norms(e):
                pe.wait_ge(s_sq2, e + 1)
                if e:
                    pe.wait_ge(s_s, e)
                mm(bank[2][:, 2 * e:2 * e + 2], ones[:], wss[:, e], start=True, stop=True).then_inc(s_sp, 1)

            def z_pair(i):
                pe.wait_ge(s_xt, i + 1)
                if i >= 2:
                    pe.wait_ge(s_zc, i - 1)
                for t in range(2):
                    for k in range(KD):
                        mm(bank[6][:, (2 * i + t) * E:(2 * i + t + 1) * E], xt_sb[:, i % 2, t, k, :],
                           wg[:, k, :], start=(k == 0), stop=(k == KD - 1))
                for t in range(2):
                    for k in range(KD):
                        last = mm(bank[i % 2][:, t * D:(t + 1) * D], xt_sb[:, i % 2, t, k, :], weff[:, k, :],
                                  start=(k == 0), stop=(k == KD - 1))
                last.then_inc(s_zpr, 1)

            x_pair(0)
            x_pair(1)
            pe.wait_ge(s_bsq, 1)
            mm(bank[2][:, 32:32 + E], ones[:], bss[:], start=True, stop=True)
            norms(0)
            pe.wait_ge(s_rt, 1)
            pe.wait_ge(s_win, 16 * 2)
            for ki in range(KD):
                for kj in range(KD):
                    mm(bank[1][:, ki * D:(ki + 1) * D], rt[:, kj, ki * P:(ki + 1) * P], winr[:, kj, :],
                       start=(kj == 0), stop=(kj == KD - 1))
            for kd in range(KD):
                for kj in range(KD):
                    last = mm(bank[6][:, kd * D:(kd + 1) * D], winr[:, kj, kd * P:(kd + 1) * P], rt[:, kj, :],
                              start=(kj == 0), stop=(kj == KD - 1))
            last.then_inc(s_wep, 1)
            pe.wait_ge(s_we, 1)
            for ki in range(KD):
                for kd in range(KD):
                    mm(bank[3][:, ki * E:(ki + 1) * E], wefft[:, kd, ki * P:(ki + 1) * P], wgr[:, kd, :],
                       start=(kd == 0), stop=(kd == KD - 1))
            pe.wait_ge(s_rep, 1)
            for kd in range(KD):
                mm(bank[3][:, 64:64 + E], binrep[:, kd, :], wgr[:, kd, :], start=(kd == 0), stop=False)
            mm(bank[3][:, 64:64 + E], ones[0:1, :], bgr[:], start=False, stop=True).then_inc(s_wgp, 1)
            pe.wait_ge(s_wg, 1)
            norms(1)
            for i in range(NT // 2):
                if 1 <= i < NT // 2 - 1:
                    x_pair(i + 1)
                z_pair(i)
                if i % 4 == 3:
                    norms(2 + i // 4)
            pe.wait_ge(s_m, 1)
            m_et = m16[:].rearrange("p e t -> p (e t)")
            mm(bank[4][:, 0:E * NT], before[:], m_et, start=True, stop=True)
            mm(bank[4][:, E * NT:2 * E * NT], ones16[:], m_et, start=True, stop=True).then_inc(s_rank, 1)
            norms(6)
            for b in range(NB):
                pe.wait_ge(s_oh, b + 1)
                pe.wait_ge(s_ohu, b + 1)
                for q in range(OB):
                    last = mm(bank[7][:, 0:2 * NA], ohb[:, b % 2, q, :],
                              oha[:, b % 2, q].rearrange("p a c -> p (a c)"),
                              start=(b == 0 and q == 0), stop=(b == NB - 1 and q == OB - 1))
                last.then_inc(s_ohp, 1)
                if b == NB - 3:
                    norms(7)

            def rows_t(a, par, j):
                pe.wait_ge(s_g[par], (j + 1) * (16 * H))
                if later(a, 2):
                    pe.wait_ge(s_xl, a - 1)
                for k in range(KD):
                    for h in range(H):
                        last = tr(XB[par][:, k * TS + h * P:k * TS + (h + 1) * P], gx[:, par, h, k * P:(k + 1) * P],
                                  ident[:])
                last.then_inc(s_tp, 1)

            def w1_at(e, l, k, c):
                return w1s[:, bass.ds(e, 1), l, k, c * P:(c + 1) * P].rearrange("p e f -> p (e f)")

            def w2_at(e, l, c):
                return w2s[:, bass.ds(e, 1), l, c, :].rearrange("p e f -> p (e f)")

            def first_layer(a, par, e):
                pe.wait_ge(s_xl, a + 1)
                for b in range(4):
                    if later(a, 1):
                        pe.wait_ge(s_mf, a * 4 + (b - 3))
                    for c in range(2):
                        o = FB[b][:, c * TS:(c + 1) * TS]
                        for k in range(KD):
                            w = w1_at(e, 0, k, 2 * b + c)
                            mm(o, w, xs[:, par, 0, k, :], start=(k == 0), stop=False)
                            mm(o, w, xs[:, par, 1, k, :], start=False, stop=False)
                            last = mm(o, w1_at(e, 1, k, 2 * b + c), xs[:, par, 0, k, :], start=False,
                                      stop=(k == KD - 1))
                    last.then_inc(s_mp, 1)

            def second_layer(a, par, e):
                if later(a, 2):
                    pe.wait_ge(s_ys, a - 1)
                for b in range(4):
                    pe.wait_ge(s_mq, a * 4 + (b + 1))
                    for c in range(2):
                        f = 2 * b + c
                        for l, w in ((0, 0), (1, 0), (0, 1)):
                            for h in range(H):
                                last = mm(YB[par][:, h * D:(h + 1) * D],
                                          mids[:, par, l, b, c * TS + h * P:c * TS + (h + 1) * P], w2_at(e, w, f),
                                          start=(f == 0 and l == 0 and w == 0 and h == 0),
                                          stop=(f == KF - 1 and w == 1), skip_group_check=True)
                last.then_inc(s_yp, 1)

            def expert(a):
                return pe.value_load(tile_e[0:1, bass.ds(a, 1)], min_val=0, max_val=E - 1)

            def tile(a, par, j):
                first_layer(a, par, expert(a))
                if not isinstance(a, int) or a < NTILE - 1:
                    rows_t(a + 1, 1 - par, j + par)
                if later(a, 1):
                    second_layer(a - 1, 1 - par, expert(a - 1))

            rows_t(0, 0, 0)
            pe.wait_ge(s_te, 1)
            pe.wait_ge(s_tab, 1)
            wait_low(pe, E - 1, 4)
            wait_low(pe, EP, 4)
            tiles(pe, tile)
            second_layer(NTILE - 1, 0, expert(NTILE - 1))

            def project(i, par):
                pe.wait_ge(s_zt, i + 1)
                if later(i, 2):
                    pe.wait_ge(s_o, i - 1)
                for t in range(CT):
                    for k in range(KD):
                        last = mm(bank[2 + par][:, t * D:(t + 1) * D], zt[:, par, t, k, :], wout[:, k, :],
                                  start=(k == 0), stop=(k == KD - 1))
                last.then_inc(s_op, 1)

            def mix_t(i, slot, j):
                pe.wait_ge(s_z, i + 1)
                if later(i, 2):
                    pe.wait_ge(s_zt, i - 1)
                for t in range(CT):
                    for k in range(KD):
                        last = tr(bank[slot % 2][:, (t * KD + k) * P:(t * KD + k + 1) * P],
                                  ztok[:, slot % 2, t, k * P:(k + 1) * P], ident[:])
                last.then_inc(s_zp, 1)
                if later(i, 1):
                    project(i - 1, (slot + 1) % 2)

            combine(pe, mix_t)
            project(NS - 1, (NS - 1) % 2)


_ARGS = ['x', 'cond_256', 'L0_cond_q_right', 'L0_cond_spectral_gate', 'L0_ffn_W_in', 'L0_ffn_b_in', 'L0_ffn_W_gate',
         'L0_ffn_b_gate', 'L0_ffn_W1', 'L0_ffn_b1', 'L0_ffn_W2', 'L0_ffn_b2', 'L0_ffn_W_out', 'L0_ffn_b_out']


def kernel(**inputs):
    import numpy as _np
    import concourse.bacc as _bacc
    from concourse import mybir as _mybir
    from concourse.bass_utils import run_bass_kernel_spmd as _run

    nc = _bacc.Bacc("TRN2", target_bir_lowering=False, num_devices=1)
    arrays, args = {}, []
    for name in _ARGS:
        a = _np.ascontiguousarray(inputs[name])
        if name == 'x':
            a = a.reshape(-1, a.shape[-1])
        if name == 'L0_cond_spectral_gate':
            a = a.reshape(1, -1)
        arrays[f"in_{name}"] = a
        args.append(nc.dram_tensor(f"in_{name}", a.shape, _mybir.dt.from_np(a.dtype), kind="ExternalInput").ap())
    shape = _np.shape(inputs['x'])
    out = nc.dram_tensor("out_0", (shape[0] * shape[1], shape[2]), _mybir.dt.float32, kind="ExternalOutput").ap()
    moe_program(nc, *args, out)
    r = _run(nc, [arrays], core_ids=[0])
    return r.results[0]["out_0"].reshape(shape)
```
